# Optimizing a Trainium2 kernel written in Bass

```python
import numpy as np
import jax
import jax.numpy as jnp

def _softmax(x, axis=-1):
    return jax.nn.softmax(x, axis=axis)

def _gelu(x):
    return jax.nn.gelu(x, approximate=True)

def _silu(x):
    return jax.nn.silu(x)

def _sigmoid(x):
    return jax.nn.sigmoid(x)

def _layernorm(x, axis=-1, eps=1e-05):
    m = jnp.mean(x, axis=axis, keepdims=True)
    v = jnp.var(x, axis=axis, keepdims=True)
    return (x - m) / jnp.sqrt(v + eps)

def _scatter_add(tgt, idx, src, axis=0):
    return tgt.at[idx].add(src)

def _segment_sum(src, seg, n):
    return jax.ops.segment_sum(src, seg, n)
kernel_name = 'mk_flamingo_gated_d1_seqx_r4_17a505'

def setup_inputs(seed: int=0):
    np.random.seed(seed)
    _w = jnp.asarray

    def _rec_inputs():
        import jax
        import jax.numpy as jnp
        _rk = jax.random.key(seed)
        x = 7.22e-05 + 1 * jax.random.normal(jax.random.fold_in(_rk, 1), (8, 112, 256), jnp.float32)
        _lenS = 112 - jax.random.randint(jax.random.fold_in(_rk, 7), (8,), 0, max(1, 112 // 4) + 1, jnp.int32)
        _lenS2 = 375 - jax.random.randint(jax.random.fold_in(_rk, 8), (8,), 0, max(1, 375 // 4) + 1, jnp.int32)
        _ctx_1024P = jax.random.normal(jax.random.fold_in(_rk, 11), (8, 16, 256), jnp.float32)
        _ctx_1024c = jax.random.dirichlet(jax.random.fold_in(_rk, 511), 0.3 * jnp.ones((16,), jnp.float32), (8, 375))
        _ctx_1024t = jnp.einsum('bsk,bkd->bsd', _ctx_1024c, _ctx_1024P)
        _ctx_1024t = _ctx_1024t * jax.lax.rsqrt(jnp.mean(jnp.square(_ctx_1024t)) + 1e-12) * 0.953939
        ctx_1024 = -4.77421e-07 + 0.031248 * (_ctx_1024t + 0.3 * jax.random.normal(jax.random.fold_in(_rk, 611), (8, 375, 256), jnp.float32))
        _g = jax.random.normal(jax.random.fold_in(_rk, 9001), (2, 1), jnp.float32)
        _g = jnp.sign(_g) * jnp.maximum(jnp.abs(_g), 1.0) + (_g == 0) * 1.0
        g_xattn = _g[0]
        g_ffn = _g[1]
        return (x, ctx_1024, g_xattn, g_ffn)
    x, ctx_1024, g_xattn, g_ffn = _rec_inputs()

    def _L0_xattn_setup():
        import jax, jax.numpy as jnp
        import numpy as np
        E, T, H, F = (8, 256, 256, 1024)
        key = jax.random.key(seed)
        k1, k2, k3 = jax.random.split(key, 3)
        x = jax.random.normal(k1, (E, T, H), dtype=jnp.float32)
        w1 = jax.random.normal(k2, (E, F, H), dtype=jnp.float32) * (1.0 / np.sqrt(H))
        w2 = jax.random.normal(k3, (E, F, H), dtype=jnp.float32) * (1.0 / np.sqrt(F))
        return {'x': x, 'w1': w1, 'w2': w2}
    _L0_xattn_all = _L0_xattn_setup()
    _L0_xattn_in = {k: v for k, v in _L0_xattn_all.items() if k in ()}
    del _L0_xattn_all

    def _L0_ffn_setup():
        import jax, jax.numpy as jnp
        import numpy as np
        B, S, D, H, E = (4, 512, 256, 1024, 8)
        key = jax.random.key(seed)
        ks = jax.random.split(key, 8)
        s_d = 1.0 / np.sqrt(D)
        s_h = 1.0 / np.sqrt(H)
        return {'x': jax.random.normal(ks[0], (B, S, D), dtype=jnp.float32), 'gate_w': jax.random.uniform(ks[1], (E, D), jnp.float32, -s_d, s_d), 'gate_b': jax.random.uniform(ks[2], (E,), jnp.float32, -s_d, s_d), 'w1': jax.random.uniform(ks[3], (E, H, D), jnp.float32, -s_d, s_d), 'b1': jax.random.uniform(ks[4], (E, H), jnp.float32, -s_d, s_d), 'w2': jax.random.uniform(ks[5], (E, D, H), jnp.float32, -s_h, s_h), 'b2': jax.random.uniform(ks[6], (E, D), jnp.float32, -s_h, s_h)}
    _L0_ffn_all = _L0_ffn_setup()
    _L0_ffn_in = {k: v for k, v in _L0_ffn_all.items() if k in ('gate_w', 'gate_b', 'w1', 'b1', 'w2', 'b2')}
    del _L0_ffn_all
    return {'x': x, 'ctx_1024': ctx_1024, 'g_xattn': g_xattn, 'g_ffn': g_ffn, 'L0_ffn_gate_w': _L0_ffn_in['gate_w'], 'L0_ffn_gate_b': _L0_ffn_in['gate_b'], 'L0_ffn_w1': _L0_ffn_in['w1'], 'L0_ffn_b1': _L0_ffn_in['b1'], 'L0_ffn_w2': _L0_ffn_in['w2'], 'L0_ffn_b2': _L0_ffn_in['b2']}

def reference(x, ctx_1024, g_xattn, g_ffn, L0_ffn_gate_w, L0_ffn_gate_b, L0_ffn_w1, L0_ffn_b1, L0_ffn_w2, L0_ffn_b2):
    import jax
    import jax.numpy as jnp

    def _L0_xattn_ref(x, w1, w2):
        import jax, jax.numpy as jnp
        import numpy as np
        E, T, H, F = (8, 256, 256, 1024)
        h = jnp.einsum('eth,efh->etf', x, w1)
        g = jax.nn.gelu(h, approximate=True)
        out = jnp.einsum('etf,efh->eth', g, w2)
        return out

    def _L0_ffn_ref(x, gate_w, gate_b, w1, b1, w2, b2):
        import jax, jax.numpy as jnp
        import numpy as np
        B, S, D, H, E = (4, 512, 256, 1024, 8)
        b, s, d = x.shape
        xf = x.reshape(-1, d)
        logits = xf @ gate_w.T + gate_b
        top1 = jnp.argmax(logits, axis=-1)
        out = jnp.zeros_like(xf)
        n_experts = w1.shape[0]
        for e in range(n_experts):
            h = jax.nn.relu(xf @ w1[e].T + b1[e])
            y = h @ w2[e].T + b2[e]
            out = out + jnp.where((top1 == e)[:, None], y, jnp.zeros((), y.dtype))
        return out.reshape(b, s, d)
    x = x + jnp.tanh(g_xattn[0]) * _L0_xattn_ref(_layernorm(x, axis=-1), ctx_1024, ctx_1024)
    x = x + jnp.tanh(g_ffn[0]) * _L0_ffn_ref(_layernorm(x, axis=-1), L0_ffn_gate_w, L0_ffn_gate_b, L0_ffn_w1, L0_ffn_b1, L0_ffn_w2, L0_ffn_b2)
    return x

_drawn_inputs = setup_inputs


def setup_inputs(seed=0):
    import zlib

    import numpy as np

    out = dict(_drawn_inputs(seed))
    spreads = {}
    factors = {'L0_ffn_b1': 5.832, 'L0_ffn_b2': 4.603}
    for name, (base, spread) in spreads.items():
        noise = np.random.default_rng([zlib.crc32(name.encode()), seed]).standard_normal(out[name].shape)
        drawn = base * np.exp(spread * noise) if base else spread * noise
        out[name] = jnp.asarray(drawn.astype(out[name].dtype))
    for name, factor in factors.items():
        out[name] = (out[name] * factor).astype(out[name].dtype)
    return out
```

```python
from contextlib import ExitStack

import concourse.bass as bass
from concourse import mybir

P = 128
ALU = mybir.AluOpType
ACT = mybir.ActivationFunctionType
AX_X = mybir.AxisListType.X
F32 = mybir.dt.float32
BF16 = mybir.dt.bfloat16
I32 = mybir.dt.int32
U32 = mybir.dt.uint32

EPS = 1e-5
B, S, D = 8, 112, 256
CTX = 375
E, H = 8, 1024
TOKENS = B * S
KD, KH = D // P, H // P
CC, CR = 3, CTX // 3
ROW = D + 4
MEAN, VAR, RSTD, VEPS = D, D + 1, D + 2, D + 3
CHUNKS = TOKENS // P
MAX_OVER = CHUNKS - 1
SLOTS = CHUNKS * E
NOWHERE = 65536.0


def gated_cross_attention_moe(nc, x, ctx_rows, ctx_cols, g_attn, g_ffn, gate_wt, gate_b,
                              w1t, b1t, w2t, b2, out):
    x2_dram = nc.dram_tensor("x2_rows", (TOKENS, ROW), F32, kind="Internal").ap()
    with ExitStack() as stack:
        def sb(name, shape, dt=F32):
            return stack.enter_context(nc.sbuf_tensor(name, shape, dt))

        def ps(name, shape):
            return stack.enter_context(nc.psum_tensor(name, shape, F32))

        def sem(name):
            return stack.enter_context(nc.semaphore(name))

        w1 = sb("w1", [P, E, KD * H])
        w2 = sb("w2", [P, E, KH * D])
        b1 = sb("b1", [P, E * KH])
        b2b = sb("b2b", [P, E * D])
        gw = sb("gw", [P, KD * E])
        gb = sb("gb", [P, E])
        gates = sb("gates", [P, 2])
        tg = sb("tg", [P, 2])
        region = sb("region", [P, B * (KD * CTX + CC * D)])
        cxT = region[:, 0:B * KD * CTX].rearrange("p (b n) -> p b n", b=B)
        cx = region[:, B * KD * CTX:].rearrange("p (b n) -> p b n", b=B)
        hid = region[:, 0:2 * H].rearrange("p (q n) -> p q n", q=2)
        hidT = region[:, 2 * H:3 * H].rearrange("p (k n) -> p k n", k=KH)
        xg = region[:, 3 * H:3 * H + (E + 2) * ROW].rearrange("p (j n) -> p j n", j=E + 2)
        xgn = region[:, 6 * H:6 * H + 2 * D].rearrange("p (q n) -> p q n", q=2)
        xgT = region[:, 6 * H + 2 * D:6 * H + 4 * D].rearrange("p (q n) -> p q n", q=2)

        xn = w1[:, E - 1, 0:2 * D].rearrange("p (q n) -> p q n", q=2)
        xn2 = w2[:, E - 1, 0:2 * D].rearrange("p (q n) -> p q n", q=2)
        gel = w2[:, E - 1, 2 * D:2 * D + 2 * CTX].rearrange("p (q n) -> p q n", q=2)
        gelT = w2[:, E - 1, 1280:1280 + 2 * CC * S].rearrange("p (q n) -> p q n", q=2)

        xs = sb("xs", [P, B, D])
        x2 = sb("x2", [P, 2, ROW])
        xnT = sb("xnT", [P, 2, KD * S])
        xn2T = sb("xn2T", [P, 2, KD * S])
        stats = sb("stats", [P, 6])
        stats2 = sb("stats2", [P, 6])
        mv = sb("mv", [P, 2, 4])
        power = sb("power", [P, 1])
        eps = sb("eps", [P, 1])

        ident = sb("ident", [P, P])
        tri = sb("tri", [P, S], BF16)
        ones = sb("ones", [P, P], BF16)
        iota_r = sb("iota_r", [P, P], BF16)
        iota_e = sb("iota_e", [P, E])
        iota_k = sb("iota_k", [P, SLOTS])
        iota_b = sb("iota_b", [P, B])
        iota_j = sb("iota_j", [P, MAX_OVER])
        row_1 = sb("row_1", [P, 1])
        upto = sb("upto", [P, E, E])

        lg = sb("lg", [P, B, E])
        eq = sb("eq", [P, B, E])
        cand = sb("cand", [P, B, E])
        mx = sb("mx", [P, B])
        first = sb("first", [P, B])
        oh = sb("oh", [P, B, E], BF16)
        rk = sb("rk", [P, B, E])
        rank = sb("rank", [P, B])
        rank_i = sb("rank_i", [P, B], I32)
        rmod = sb("rmod", [P, B])
        base = sb("base", [P, B], I32)
        key = sb("key", [P, B])
        pick_r = sb("pick_r", [P, B, P], BF16)
        pick_k = sb("pick_k", [P, B, 2 * SLOTS], BF16)
        id1 = sb("id1", [P, SLOTS])
        empty = sb("empty", [P, SLOTS])
        from_row = sb("from_row", [P, SLOTS], U32)
        to_row = sb("to_row", [P, SLOTS], U32)
        from_over = sb("from_over", [P, 2], U32)
        to_over = sb("to_over", [P, 2], U32)
        flags = sb("flags", [P, E, MAX_OVER])
        over = sb("over", [P, E])
        cum2 = sb("cum2", [P, E, E])
        cum = sb("cum", [P, E])
        before = sb("before", [P, MAX_OVER, E])
        before_n = sb("before_n", [P, MAX_OVER, E])
        ej = sb("ej", [P, MAX_OVER])
        sj = sb("sj", [P, MAX_OVER])
        cj = sb("cj", [P, MAX_OVER])
        ctrl = sb("ctrl", [P, 2 * MAX_OVER + 1], I32)

        banks = [ps(f"bank{i}", [P, 512]) for i in range(8)]
        xnT_ps, sc_ps, gelT_ps, at_ps, xn2T_ps = banks[0:5]
        cnt_ps, lg_ps, rk_ps, tok_ps = banks[5], banks[6], banks[7], banks[0]
        h_ps = banks[0:2]
        hT_ps = banks[2:6]
        y_ps, xgT_ps = banks[6], banks[7]

        x0_in, x_in = sem("x0_in"), sem("x_in")
        g_in, small_in, b2_in = sem("g_in"), sem("small_in"), sem("b2_in")
        ctx_in = [sem("ctx_in0"), sem("ctx_in1")]
        w1_in = [sem("w1_in0"), sem("w1_in1")]
        w2_in = [sem("w2_in0"), sem("w2_in1")]
        pool_step = sem("pool_step")
        ident_ok, consts_ok = sem("ident_ok"), sem("consts_ok")
        tg_ok, veps_ok = sem("tg_ok"), sem("veps_ok")
        s1_ok, stats_ok, rstd_ok, xn_ok = sem("s1_ok"), sem("stats_ok"), sem("rstd_ok"), sem("xn_ok")
        xnT_done, xnT_ok = sem("xnT_done"), sem("xnT_ok")
        sc_done, gel_ok = sem("sc_done"), sem("gel_ok")
        gelT_done, gelT_ok = sem("gelT_done"), sem("gelT_ok")
        at_done, x2_ok = sem("at_done"), sem("x2_ok")
        s2_ok, stats2_ok, rstd2_ok, xn2_ok = sem("s2_ok"), sem("stats2_ok"), sem("rstd2_ok"), sem("xn2_ok")
        xn2T_done, xn2T_ok, lg_done = sem("xn2T_done"), sem("xn2T_ok"), sem("lg_done")
        x2_stored = [sem("x2_stored0"), sem("x2_stored1")]
        dve_step = sem("dve_step")
        oh_ok, rk_done, picks_ok, tok_done = sem("oh_ok"), sem("rk_done"), sem("picks_ok"), sem("tok_done")
        rows_ok, ctrl_ok = sem("rows_ok"), sem("ctrl_ok")
        cnt_done, cnt_read = sem("cnt_done"), sem("cnt_read")
        xg_in = [sem("xg_in0"), sem("xg_in1")]
        over_in = [sem("over_in0"), sem("over_in1")]
        over_idx = sem("over_idx")
        xgn_ok, xgT_done, xgT_ok = sem("xgn_ok"), sem("xgT_done"), sem("xgT_ok")
        h_done = sem("h_done")
        h0_ok, h1_ok = sem("h0_ok"), sem("h1_ok")
        hT_done = sem("hT_done")
        hTa_ok, hTd_ok = sem("hTa_ok"), sem("hTd_ok")
        y_done, yb_ok, o_ok = sem("y_done"), sem("yb_ok"), sem("o_ok")
        out_done = [sem("out_done0"), sem("out_done1")]

        block = stack.enter_context(nc.Block())

        @block.sync
        def _(sp):
            def load_context(b, q):
                sp.dma_start(cxT[:, b, :], ctx_cols[b]).then_inc(ctx_in[q], 16)
                sp.dma_start(cx[0:CR, b, :].rearrange("p (c d) -> p c d", c=CC),
                             ctx_rows[b].rearrange("(c p) d -> p c d", p=CR)).then_inc(ctx_in[q], 16)

            def load_expert(e, q):
                sp.dma_start(w1[:, e, :], w1t[e]).then_inc(w1_in[q], 16)
                sp.dma_start(w2[:, e, :], w2t[e]).then_inc(w2_in[q], 16)

            for b in range(2):
                load_context(b, b)
            with sp.Fori(1, B // 2) as t:
                for q in range(2):
                    sp.wait_ge(ctx_in[q], 32 * t)
                    load_context(2 * t + q, q)
            for e in range(2):
                load_expert(e, e)
            with sp.Fori(1, E // 2 - 1) as t:
                for q in range(2):
                    sp.wait_ge(w1_in[q], 16 * t)
                    sp.wait_ge(w2_in[q], 16 * t)
                    load_expert(2 * t + q, q)
            sp.wait_ge(w1_in[0], 16 * (E // 2 - 1))
            sp.wait_ge(w2_in[0], 16 * (E // 2 - 1))
            load_expert(E - 2, 0)
            sp.wait_ge(lg_done, B)
            sp.wait_ge(w1_in[1], 16 * (E // 2 - 1))
            sp.wait_ge(w2_in[1], 16 * (E // 2 - 1))
            load_expert(E - 1, 1)

        @block.gpsimd
        def _(pool):
            pool.memset(ident[:], 0.0).then_inc(pool_step, 1)
            pool.wait_ge(pool_step, 1)
            pool.affine_select(out=ident[:], in_=ident[:], compare_op=ALU.not_equal, fill=1.0, base=0,
                               pattern=[[-1, P]], channel_multiplier=1).then_inc(ident_ok, 1)
            pool.memset(power[:], -0.5).then_inc(pool_step, 1)
            pool.memset(eps[:], EPS).then_inc(pool_step, 1)
            pool.memset(ones[:], 1.0).then_inc(pool_step, 1)
            pool.wait_ge(pool_step, 4)
            pool.affine_select(out=tri[:], in_=ones[:, 0:S], compare_op=ALU.is_gt, fill=0.0, base=0,
                               pattern=[[1, S]], channel_multiplier=-1).then_inc(consts_ok, 1)
            pool.iota(iota_r[:], [[1, P]], base=0, channel_multiplier=0,
                      allow_small_or_imprecise_dtypes=True).then_inc(consts_ok, 1)
            pool.iota(iota_e[:], [[1, E]], base=-E, channel_multiplier=0,
                      allow_small_or_imprecise_dtypes=True).then_inc(consts_ok, 1)
            pool.iota(iota_k[:], [[P, SLOTS]], base=-P * E, channel_multiplier=0,
                      allow_small_or_imprecise_dtypes=True).then_inc(consts_ok, 1)
            pool.iota(iota_b[:], [[1, B]], base=0, channel_multiplier=0,
                      allow_small_or_imprecise_dtypes=True).then_inc(consts_ok, 1)
            pool.iota(iota_j[:], [[1, MAX_OVER]], base=0, channel_multiplier=0,
                      allow_small_or_imprecise_dtypes=True).then_inc(consts_ok, 1)
            pool.iota(row_1[:], [[0, 1]], base=1, channel_multiplier=1,
                      allow_small_or_imprecise_dtypes=True).then_inc(consts_ok, 1)
            pool.memset(upto[:], 1.0).then_inc(pool_step, 1)
            pool.wait_ge(pool_step, 5)
            pool.affine_select(out=upto[:], in_=upto[:], compare_op=ALU.is_ge, fill=0.0, base=0,
                               pattern=[[1, E], [-1, E]], channel_multiplier=0).then_inc(consts_ok, 1)
            def inverse_std(v, count):
                pool.tensor_tensor(v[:, 3:4], v[:, 1:2], eps[0:S, :], ALU.add).then_inc(veps_ok, 1)
                pool.wait_ge(veps_ok, count)
                return pool.tensor_tensor(v[:, 2:3], v[:, 3:4], power[0:S, :], ALU.pow)

            def of_x(b, q, count):
                pool.wait_ge(stats_ok, b + 1)
                inverse_std(mv[0:S, q, :], count).then_inc(rstd_ok, 1)

            def of_x2(b, q, count):
                pool.wait_ge(stats2_ok, b + 1)
                inverse_std(x2[0:S, q, MEAN:], count).then_inc(rstd2_ok, 1)

            of_x(0, 0, 1)
            of_x(1, 1, 2)
            with pool.Fori(0, B // 2 - 1) as t:
                for q in range(2):
                    b = 2 * t + q
                    of_x(b + 2, q, 2 * b + 3)
                    of_x2(b, q, 2 * b + 4)
            of_x2(B - 2, 0, 2 * B - 1)
            of_x2(B - 1, 1, 2 * B)

            pool.wait_ge(rows_ok, 2)
            for q in range(2):
                pool.wait_ge(x2_stored[q], 16 * B // 2)
            for e in range(E):
                if e >= 2:
                    pool.wait_ge(xg_in[e % 2], 16 * (e // 2))
                pool.indirect_dma_start(
                    out=xg[:, e, :], out_offset=None, in_=x2_dram,
                    in_offset=bass.IndirectOffsetOnAxis(ap=from_row[:, e:e + 1], axis=0),
                    bounds_check=TOKENS - 1, oob_is_err=False).then_inc(xg_in[e % 2], 16)

            pool.wait_ge(ctrl_ok, 1)
            n_over = pool.value_load(ctrl[0:1, 2 * MAX_OVER:2 * MAX_OVER + 1], min_val=0, max_val=MAX_OVER)

            def over_gather(m, q):
                col = pool.value_load(ctrl[0:1, bass.ds(MAX_OVER + m, 1)], min_val=0, max_val=SLOTS - 1)
                pool.tensor_copy(from_over[:, q:q + 1], from_row[:, bass.ds(col, 1)]).then_inc(over_idx, 1)
                pool.tensor_copy(to_over[:, q:q + 1], to_row[:, bass.ds(col, 1)]).then_inc(over_idx, 1)
                pool.wait_ge(over_idx, 2 * (m + 1))
                pool.indirect_dma_start(
                    out=xg[:, E + q, :], out_offset=None, in_=x2_dram,
                    in_offset=bass.IndirectOffsetOnAxis(ap=from_over[:, q:q + 1], axis=0),
                    bounds_check=TOKENS - 1, oob_is_err=False).then_inc(over_in[q], 16)

            with pool.If(n_over > 0):
                over_gather(0, 0)
            for e in range(E):
                pool.wait_ge(o_ok, e + 1)
                pool.indirect_dma_start(
                    out=out, out_offset=bass.IndirectOffsetOnAxis(ap=to_row[:, e:e + 1], axis=0),
                    in_=xg[:, e, 0:D], in_offset=None,
                    bounds_check=TOKENS - 1, oob_is_err=False).then_inc(out_done[0], 16)
            for m in range(MAX_OVER):
                q = m % 2
                with pool.If(n_over > m):
                    pool.wait_ge(o_ok, E + 1 + m)
                    pool.indirect_dma_start(
                        out=out, out_offset=bass.IndirectOffsetOnAxis(ap=to_over[:, q:q + 1], axis=0),
                        in_=xg[:, E + q, 0:D], in_offset=None,
                        bounds_check=TOKENS - 1, oob_is_err=False).then_inc(out_done[1], 16)
                    pool.wait_ge(out_done[1], 16 * (m + 1))
                if m + 1 < MAX_OVER:
                    with pool.If(n_over > m + 1):
                        over_gather(m + 1, 1 - q)
            pool.wait_ge(out_done[0], 16 * E)

        @block.scalar
        def _(act):
            act.dma_start(xs[0:S, 0, :], x[0:S]).then_inc(x0_in, 16)
            act.dma_start(xs[0:S, 1:B, :],
                          x[S:TOKENS].rearrange("(b p) d -> p b d", p=S)).then_inc(x_in, 16)
            act.dma_start(gates[:, 0:1], g_attn.partition_broadcast(P)).then_inc(g_in, 16)
            act.dma_start(gates[:, 1:2], g_ffn.partition_broadcast(P)).then_inc(g_in, 16)
            act.dma_start(gw[:], gate_wt).then_inc(small_in, 16)
            act.dma_start(gb[:], gate_b.partition_broadcast(P)).then_inc(small_in, 16)
            act.dma_start(b1[:], b1t).then_inc(small_in, 16)
            act.wait_ge(g_in, 32)
            act.activation(tg[:], gates[:], ACT.Tanh).then_inc(tg_ok, 1)

            def xnT_copy(b, q):
                act.wait_ge(xnT_done, b + 1)
                act.activation(xnT[:, q, :], xnT_ps[:, 0:KD * S], ACT.Copy).then_inc(xnT_ok, 1)

            def gelu(b, q):
                act.wait_ge(sc_done, b + 1)
                act.activation(gel[0:S, q, 0:CTX], sc_ps[0:S, 0:CTX], ACT.Gelu_apprx_tanh).then_inc(gel_ok, 1)

            def gelT_copy(b, q):
                act.wait_ge(gelT_done, b + 1)
                act.activation(gelT[0:CR, q, :], gelT_ps[0:CR, 0:CC * S], ACT.Copy).then_inc(gelT_ok, 1)

            def xn2T_copy(b, q):
                act.wait_ge(xn2T_done, b + 1)
                act.activation(xn2T[:, q, :], xn2T_ps[:, 0:KD * S], ACT.Copy).then_inc(xn2T_ok, 1)
                act.wait_ge(rstd2_ok, b + 1)
                act.dma_start(x2_dram[bass.ds(b * S, S), :], x2[0:S, q, :]).then_inc(x2_stored[q], 16)

            xnT_copy(0, 0)
            gelu(0, 0)
            xnT_copy(1, 1)
            gelT_copy(0, 0)
            gelu(1, 1)
            with act.Fori(0, B // 2 - 1) as t:
                for r in range(2):
                    b, q = 2 * t + 1 + r, (1 + r) % 2
                    xnT_copy(b + 1, 1 - q)
                    gelT_copy(b, q)
                    gelu(b + 1, 1 - q)
                    xn2T_copy(b - 1, 1 - q)
            gelT_copy(B - 1, 1)
            act.dma_start(b2b[:], b2.partition_broadcast(P)).then_inc(b2_in, 16)
            xn2T_copy(B - 2, 0)
            xn2T_copy(B - 1, 1)

            def xgT_copy(j, q):
                act.wait_ge(xgT_done, j + 1)
                act.activation(xgT[:, q, :], xgT_ps[:, 0:D], ACT.Copy).then_inc(xgT_ok, 1)

            def h0_copy(j, q):
                act.wait_ge(h_done, 2 * j + 1)
                act.activation(hid[:, q, 0:H // 2], h_ps[0][:], ACT.Copy).then_inc(h0_ok, 1)

            def relu(j, e):
                for k in (0, 2):
                    act.wait_ge(hT_done, 4 * j + k + 1)
                    for r in range(2):
                        act.activation(hidT[:, 2 * k + r, :], hT_ps[k][:, r * P:(r + 1) * P], ACT.Relu,
                                       bias=b1[:, bass.ds(e * KH + 2 * k + r, 1)]).then_inc(hTa_ok, 1)

            act.wait_ge(small_in, 48)
            xgT_copy(0, 0)
            h0_copy(0, 0)
            xgT_copy(1, 1)
            with act.Fori(0, E // 2 - 1) as t:
                for q in range(2):
                    j = 2 * t + q
                    h0_copy(j + 1, 1 - q)
                    xgT_copy(j + 2, q)
                    relu(j, j)
            h0_copy(E - 1, 1)
            relu(E - 2, E - 2)
            relu(E - 1, E - 1)
            act.wait_ge(ctrl_ok, 1)
            n_over = act.value_load(ctrl[0:1, 2 * MAX_OVER:2 * MAX_OVER + 1], min_val=0, max_val=MAX_OVER)
            with act.Fori(0, MAX_OVER // 2) as t:
                for q in range(2):
                    m = 2 * t + q
                    with act.If(n_over > m):
                        e = act.value_load(ctrl[0:1, bass.ds(m, 1)], min_val=0, max_val=E - 1)
                        xgT_copy(E + m, q)
                        h0_copy(E + m, q)
                        relu(E + m, e)

        @block.vector
        def _(dve):
            def norm_x(b, q, turned=None):
                dve.bn_stats(stats[0:S, :], xs[0:S, b, :]).then_inc(s1_ok, 1)
                dve.wait_ge(s1_ok, b + 1)
                dve.bn_aggr(mv[0:S, q, 0:2], stats[0:S, :]).then_inc(stats_ok, 1)
                if turned is not None:
                    dve.wait_ge(xnT_done, turned)
                dve.wait_ge(rstd_ok, b + 1)
                dve.tensor_scalar(xn[0:S, q, :], xs[0:S, b, :], mv[0:S, q, 0:1], mv[0:S, q, 2:3],
                                  ALU.subtract, ALU.mult).then_inc(xn_ok, 1)

            def residual(b, q):
                dve.wait_ge(at_done, b + 1)
                dve.scalar_tensor_tensor(out=x2[0:S, q, 0:D], in0=at_ps[0:S, 0:D], scalar=tg[0:S, 0:1],
                                         in1=xs[0:S, b, :], op0=ALU.mult, op1=ALU.add).then_inc(x2_ok, 1)

            def norm_x2(b, q):
                dve.wait_ge(x2_ok, b + 1)
                dve.bn_stats(stats2[0:S, :], x2[0:S, q, 0:D]).then_inc(s2_ok, 1)
                dve.wait_ge(s2_ok, b + 1)
                dve.bn_aggr(x2[0:S, q, MEAN:MEAN + 2], stats2[0:S, :]).then_inc(stats2_ok, 1)
                dve.wait_ge(rstd2_ok, b + 1)
                dve.tensor_scalar(xn2[0:S, q, :], x2[0:S, q, 0:D], x2[0:S, q, MEAN:MEAN + 1],
                                  x2[0:S, q, RSTD:RSTD + 1], ALU.subtract, ALU.mult).then_inc(xn2_ok, 1)

            dve.wait_ge(x0_in, 16)
            norm_x(0, 0)
            dve.wait_ge(x_in, 16)
            norm_x(1, 1)
            dve.wait_ge(tg_ok, 1)
            for b in range(B):
                if b + 2 < B:
                    norm_x(b + 2, b % 2, b + 1)
                if b >= 2:
                    dve.wait_ge(x2_stored[b % 2], 16 * (b // 2))
                    dve.wait_ge(xn2T_done, b - 1)
                residual(b, b % 2)
                norm_x2(b, b % 2)

            steps = [0]

            def step(instruction):
                instruction.then_inc(dve_step, 1)
                steps[0] += 1
                dve.wait_ge(dve_step, steps[0])

            def over_b(v):
                return v.unsqueeze(2).to_broadcast([S, B, E])

            def over_e(v):
                return v.unsqueeze(1).to_broadcast([S, B, E])

            dve.wait_ge(small_in, 48)
            dve.wait_ge(consts_ok, 8)
            dve.wait_ge(lg_done, B)
            step(dve.tensor_tensor(lg[0:S], lg_ps[0:S, 0:B * E].rearrange("p (b e) -> p b e", b=B), over_e(gb[0:S, :]), ALU.add))
            step(dve.tensor_reduce(mx[0:S], lg[0:S], AX_X, ALU.max))
            step(dve.tensor_tensor(eq[0:S], lg[0:S], over_b(mx[0:S, :]), ALU.is_equal))
            step(dve.scalar_tensor_tensor(out=cand[0:S], in0=eq[0:S], scalar=-float(E), in1=over_e(iota_e[0:S, :]),
                                          op0=ALU.mult, op1=ALU.add))
            step(dve.tensor_reduce(first[0:S], cand[0:S], AX_X, ALU.min))
            step(dve.tensor_scalar(first[0:S], first[0:S], float(E), None, ALU.add))
            dve.tensor_tensor(oh[0:S], over_e(iota_e[0:S, :]), over_b(first[0:S, :]), ALU.is_equal).then_inc(oh_ok, 1)
            dve.wait_ge(oh_ok, 1)
            dve.wait_ge(rk_done, 1)
            step(dve.tensor_tensor(rk[0:S], rk_ps[0:S, 0:B * E].rearrange("p (b e) -> p b e", b=B), oh[0:S], ALU.mult))
            step(dve.tensor_reduce(rank[0:S], rk[0:S], AX_X, ALU.add))
            step(dve.tensor_copy(rank_i[0:S], rank[0:S]))
            step(dve.tensor_scalar(base[0:S], rank_i[0:S], 7, 7, ALU.arith_shift_right, ALU.logical_shift_left))
            dve.tensor_tensor(rmod[0:S], rank[0:S], base[0:S], ALU.subtract)
            step(dve.tensor_scalar(key[0:S], base[0:S], float(E), None, ALU.mult))
            step(dve.scalar_tensor_tensor(out=key[0:S], in0=first[0:S], scalar=float(P), in1=key[0:S],
                                          op0=ALU.mult, op1=ALU.add))
            for b in range(B):
                dve.tensor_scalar(pick_r[0:S, b, :], iota_r[0:S, :], rmod[0:S, b:b + 1], None,
                                  ALU.is_equal)
            step(dve.tensor_tensor(pick_k[0:S, :, 0:SLOTS], iota_k[0:S, :].unsqueeze(1).to_broadcast([S, B, SLOTS]),
                                   key[0:S, :].unsqueeze(2).to_broadcast([S, B, SLOTS]), ALU.is_equal))
            step(dve.tensor_tensor(pick_k[0:S, :, SLOTS:2 * SLOTS], pick_k[0:S, :, 0:SLOTS],
                                   iota_b[0:S, :].unsqueeze(2).to_broadcast([S, B, SLOTS]), ALU.mult))
            dve.tensor_scalar(pick_k[0:S, :, 0:SLOTS], pick_k[0:S, :, 0:SLOTS], row_1[0:S, 0:1], None,
                              ALU.mult).then_inc(picks_ok, 1)
            dve.wait_ge(tok_done, 1)
            step(dve.tensor_copy(id1[:], tok_ps[:, 0:SLOTS]))
            step(dve.scalar_tensor_tensor(out=id1[:], in0=tok_ps[:, SLOTS:2 * SLOTS], scalar=float(S), in1=id1[:],
                                          op0=ALU.mult, op1=ALU.add))
            dve.tensor_scalar(from_row[:], id1[:], -1.0, 0.0, ALU.add, ALU.max).then_inc(rows_ok, 1)
            step(dve.tensor_scalar(empty[:], id1[:], 0.0, NOWHERE, ALU.is_equal, ALU.mult))
            dve.scalar_tensor_tensor(out=to_row[:], in0=id1[:], scalar=-1.0, in1=empty[:], op0=ALU.add,
                                     op1=ALU.add).then_inc(rows_ok, 1)

            dve.wait_ge(cnt_done, 1)
            for c in range(MAX_OVER):
                last = dve.tensor_scalar(flags[:, :, c], cnt_ps[:, 0:E], float(P * (c + 1)), None, ALU.is_gt)
            last.then_inc(cnt_read, 1)
            dve.wait_ge(cnt_read, 1)
            step(dve.tensor_reduce(over[:], flags[:], AX_X, ALU.add))
            step(dve.tensor_tensor(cum2[:], upto[:], over[:].unsqueeze(1).to_broadcast([P, E, E]), ALU.mult))
            step(dve.tensor_reduce(cum[:], cum2[:], AX_X, ALU.add))
            step(dve.tensor_tensor(before[:], cum[:].unsqueeze(1).to_broadcast([P, MAX_OVER, E]),
                                   iota_j[:].unsqueeze(2).to_broadcast([P, MAX_OVER, E]), ALU.is_le))
            step(dve.tensor_reduce(ej[:], before[:], AX_X, ALU.add))
            step(dve.tensor_tensor(before_n[:], before[:], over[:].unsqueeze(1).to_broadcast([P, MAX_OVER, E]),
                                   ALU.mult))
            step(dve.tensor_reduce(sj[:], before_n[:], AX_X, ALU.add))
            step(dve.scalar_tensor_tensor(out=cj[:], in0=iota_j[:], scalar=1.0, in1=sj[:], op0=ALU.add,
                                          op1=ALU.subtract))
            step(dve.tensor_copy(ctrl[:, 0:MAX_OVER], ej[:]))
            step(dve.scalar_tensor_tensor(out=ctrl[:, MAX_OVER:2 * MAX_OVER], in0=cj[:], scalar=float(E), in1=ej[:],
                                          op0=ALU.mult, op1=ALU.add))
            dve.tensor_copy(ctrl[:, 2 * MAX_OVER:2 * MAX_OVER + 1], cum[:, E - 1:E]).then_inc(ctrl_ok, 1)

            def norm_block(j, q, rows):
                dve.tensor_scalar(xgn[:, q, :], rows[:, 0:D], rows[:, MEAN:MEAN + 1], rows[:, RSTD:RSTD + 1],
                                  ALU.subtract, ALU.mult).then_inc(xgn_ok, 1)

            def h1_copy(j, q):
                dve.wait_ge(h_done, 2 * j + 2)
                dve.tensor_copy(hid[:, q, H // 2:H], h_ps[1][:]).then_inc(h1_ok, 1)

            def relu(j, e):
                for k in (1, 3):
                    dve.wait_ge(hT_done, 4 * j + k + 1)
                    for r in range(2):
                        dve.tensor_scalar(hidT[:, 2 * k + r, :], hT_ps[k][:, r * P:(r + 1) * P],
                                          b1[:, bass.ds(e * KH + 2 * k + r, 1)], 0.0, ALU.add,
                                          ALU.max).then_inc(hTd_ok, 1)

            def finish(j, q, e, rows):
                dve.wait_ge(y_done, j + 1)
                dve.tensor_tensor(xgn_out[:, q, :], y_ps[:, 0:D], b2b[:, bass.ds(e * D, D)], ALU.add).then_inc(yb_ok, 1)
                dve.wait_ge(yb_ok, j + 1)
                dve.scalar_tensor_tensor(out=rows[:, 0:D], in0=xgn_out[:, q, :], scalar=tg[:, 1:2], in1=rows[:, 0:D],
                                         op0=ALU.mult, op1=ALU.add).then_inc(o_ok, 1)

            xgn_out = region[:, 6 * H + 4 * D:6 * H + 6 * D].rearrange("p (q n) -> p q n", q=2)
            dve.wait_ge(b2_in, 16)
            for j in range(2):
                dve.wait_ge(xg_in[j], 16)
                norm_block(j, j, xg[:, j, :])
            h1_copy(0, 0)
            with dve.Fori(0, E // 2 - 1) as t:
                for q in range(2):
                    j = 2 * t + q
                    dve.wait_ge(xg_in[q], 16 * (t + 2))
                    dve.wait_ge(xgT_done, j + 1)
                    norm_block(j + 2, q, xg[:, j + 2, :])
                    h1_copy(j + 1, 1 - q)
                    relu(j, j)
                    finish(j, q, j, xg[:, j, :])
            h1_copy(E - 1, 1)
            relu(E - 2, E - 2)
            finish(E - 2, 0, E - 2, xg[:, E - 2, :])
            relu(E - 1, E - 1)
            finish(E - 1, 1, E - 1, xg[:, E - 1, :])
            n_over = dve.value_load(ctrl[0:1, 2 * MAX_OVER:2 * MAX_OVER + 1], min_val=0, max_val=MAX_OVER)
            with dve.Fori(0, MAX_OVER // 2) as t:
                for q in range(2):
                    m = 2 * t + q
                    with dve.If(n_over > m):
                        e = dve.value_load(ctrl[0:1, bass.ds(m, 1)], min_val=0, max_val=E - 1)
                        dve.wait_ge(over_in[q], 16 * (t + 1))
                        norm_block(E + m, q, xg[:, E + q, :])
                        h1_copy(E + m, q)
                        relu(E + m, e)
                        finish(E + m, q, e, xg[:, E + q, :])

        @block.tensor
        def _(pe):
            def turn_xn(b, q):
                pe.wait_ge(xn_ok, b + 1)
                for k in range(KD):
                    mm = pe.transpose(xnT_ps[:, k * S:(k + 1) * S], xn[0:S, q, k * P:(k + 1) * P], ident[0:S, 0:S])
                mm.then_inc(xnT_done, 1)

            def scores(b, q, ctx_wait):
                pe.wait_ge(xnT_ok, b + 1)
                pe.wait_ge(ctx_in[q], ctx_wait)
                for k in range(KD):
                    mm = pe.matmul(sc_ps[0:S, 0:CTX], xnT[:, q, k * S:(k + 1) * S], cxT[:, b, k * CTX:(k + 1) * CTX],
                                   start=(k == 0), stop=(k == KD - 1))
                mm.then_inc(sc_done, 1)

            def turn_gelu(b, q):
                pe.wait_ge(gel_ok, b + 1)
                for c in range(CC):
                    mm = pe.transpose(gelT_ps[0:CR, c * S:(c + 1) * S], gel[0:S, q, c * CR:(c + 1) * CR],
                                      ident[0:S, 0:S])
                mm.then_inc(gelT_done, 1)

            def attend(b, q):
                pe.wait_ge(gelT_ok, b + 1)
                for c in range(CC):
                    mm = pe.matmul(at_ps[0:S, 0:D], gelT[0:CR, q, c * S:(c + 1) * S], cx[0:CR, b, c * D:(c + 1) * D],
                                   start=(c == 0), stop=(c == CC - 1))
                mm.then_inc(at_done, 1)

            def turn_xn2(b, q):
                pe.wait_ge(xn2_ok, b + 1)
                for k in range(KD):
                    mm = pe.transpose(xn2T_ps[:, k * S:(k + 1) * S], xn2[0:S, q, k * P:(k + 1) * P], ident[0:S, 0:S])
                mm.then_inc(xn2T_done, 1)

            def logits(b, q):
                pe.wait_ge(xn2T_ok, b + 1)
                for k in range(KD):
                    mm = pe.matmul(lg_ps[0:S, bass.ds(b * E, E)], xn2T[:, q, k * S:(k + 1) * S], gw[:, k * E:(k + 1) * E],
                                   start=(k == 0), stop=(k == KD - 1))
                mm.then_inc(lg_done, 1)

            pe.wait_ge(ident_ok, 1)
            turn_xn(0, 0)
            scores(0, 0, 32)
            turn_xn(1, 1)
            turn_gelu(0, 0)
            scores(1, 1, 32)
            attend(0, 0)
            pe.wait_ge(small_in, 48)
            with pe.Fori(0, B // 2 - 1) as t:
                for r in range(2):
                    b, q = 2 * t + 1 + r, (1 + r) % 2
                    turn_xn(b + 1, 1 - q)
                    turn_gelu(b, q)
                    scores(b + 1, 1 - q, 32 * (t + 2))
                    turn_xn2(b - 1, 1 - q)
                    attend(b, q)
                    logits(b - 1, 1 - q)
            turn_gelu(B - 1, 1)
            turn_xn2(B - 2, 0)
            attend(B - 1, 1)
            logits(B - 2, 0)
            turn_xn2(B - 1, 1)
            logits(B - 1, 1)

            pe.wait_ge(oh_ok, 1)
            pe.wait_ge(consts_ok, 8)
            flat = oh[0:S].rearrange("p b e -> p (b e)")
            pe.matmul(rk_ps[0:S, 0:B * E], tri[0:S, :], flat, start=True, stop=False)
            for s in range(1, B):
                mm = pe.matmul(rk_ps[0:S, s * E:B * E], ones[0:S, 0:S], flat[:, 0:(B - s) * E], start=False, stop=(s == B - 1))
            mm.then_inc(rk_done, 1)
            for b in range(B):
                mm = pe.matmul(cnt_ps[:, 0:E], ones[0:S, :], flat[:, b * E:(b + 1) * E], start=(b == 0),
                               stop=(b == B - 1))
            mm.then_inc(cnt_done, 1)
            pe.wait_ge(picks_ok, 1)
            for b in range(B):
                mm = pe.matmul(tok_ps[:, 0:2 * SLOTS], pick_r[0:S, b, :], pick_k[0:S, b, :], start=(b == 0), stop=(b == B - 1))
            mm.then_inc(tok_done, 1)

            def turn_block(j, q):
                pe.wait_ge(xgn_ok, j + 1)
                for k in range(KD):
                    mm = pe.transpose(xgT_ps[:, k * P:(k + 1) * P], xgn[:, q, k * P:(k + 1) * P], ident[:])
                mm.then_inc(xgT_done, 1)

            def up(j, q, e, later=True):
                pe.wait_ge(xgT_ok, j + 1)
                for n, read in enumerate((h0_ok, h1_ok)):
                    if later:
                        pe.wait_ge(read, j)
                    for k in range(KD):
                        mm = pe.matmul(h_ps[n][:], xgT[:, q, k * P:(k + 1) * P],
                                       w1[:, e, k * H + n * 512:k * H + (n + 1) * 512],
                                       start=(k == 0), stop=(k == KD - 1))
                    mm.then_inc(h_done, 1)

            def turn_hidden(j, q):
                pe.wait_ge(h0_ok, j + 1)
                pe.wait_ge(h1_ok, j + 1)
                for k in range(KH // 2):
                    for r in range(2):
                        mm = pe.transpose(hT_ps[k][:, r * P:(r + 1) * P],
                                          hid[:, q, (2 * k + r) * P:(2 * k + r + 1) * P], ident[:])
                    mm.then_inc(hT_done, 1)

            def down(j, q, e, later=True):
                if later:
                    pe.wait_ge(yb_ok, j)
                for part in range(KH):
                    pe.wait_ge((hTa_ok, hTd_ok)[part // 2 % 2], 4 * j + part // 4 * 2 + part % 2 + 1)
                    mm = pe.matmul(y_ps[:, 0:D], hidT[:, part, :], w2[:, e, part * D:(part + 1) * D],
                                   start=(part == 0), stop=(part == KH - 1))
                mm.then_inc(y_done, 1)

            pe.wait_ge(rows_ok, 2)
            turn_block(0, 0)
            pe.wait_ge(w1_in[0], 16)
            up(0, 0, 0, later=False)
            turn_block(1, 1)
            for j in range(2):
                pe.wait_ge(w1_in[1 - j], 16 * (1 + j))
                up(j + 1, 1 - j, j + 1)
                turn_block(j + 2, j)
                pe.wait_ge(cnt_read, 1)
                turn_hidden(j, j)
                pe.wait_ge(w2_in[j], 16)
                down(j, j, j, later=(j > 0))
            with pe.Fori(1, E // 2 - 1) as t:
                for q in range(2):
                    j = 2 * t + q
                    pe.wait_ge(w1_in[1 - q], 16 * (t + 1 + q))
                    up(j + 1, 1 - q, j + 1)
                    turn_block(j + 2, q)
                    turn_hidden(j, q)
                    pe.wait_ge(w2_in[q], 16 * (t + 1))
                    down(j, q, j)
            pe.wait_ge(w1_in[1], 16 * E // 2)
            up(E - 1, 1, E - 1)
            turn_hidden(E - 2, 0)
            pe.wait_ge(w2_in[0], 16 * E // 2)
            down(E - 2, 0, E - 2)
            turn_hidden(E - 1, 1)
            pe.wait_ge(w2_in[1], 16 * E // 2)
            down(E - 1, 1, E - 1)
            pe.wait_ge(ctrl_ok, 1)
            n_over = pe.value_load(ctrl[0:1, 2 * MAX_OVER:2 * MAX_OVER + 1], min_val=0, max_val=MAX_OVER)
            with pe.Fori(0, MAX_OVER // 2) as t:
                for q in range(2):
                    m = 2 * t + q
                    with pe.If(n_over > m):
                        e = pe.value_load(ctrl[0:1, bass.ds(m, 1)], min_val=0, max_val=E - 1)
                        turn_block(E + m, q)
                        up(E + m, q, e)
                        turn_hidden(E + m, q)
                        down(E + m, q, e)


def kernel(x, ctx_1024, g_xattn, g_ffn, L0_ffn_gate_w, L0_ffn_gate_b, L0_ffn_w1, L0_ffn_b1, L0_ffn_w2, L0_ffn_b2):
    import numpy as np
    import concourse.bacc as bacc
    from concourse.bass_utils import run_bass_kernel_spmd

    arrays = {
        "x": np.ascontiguousarray(x).reshape(TOKENS, D),
        "ctx_rows": np.ascontiguousarray(ctx_1024),
        "ctx_cols": np.ascontiguousarray(
            np.asarray(ctx_1024).transpose(0, 2, 1).reshape(B, KD, P, CTX).transpose(0, 2, 1, 3)).reshape(B, P, KD * CTX),
        "g_attn": np.ascontiguousarray(g_xattn),
        "g_ffn": np.ascontiguousarray(g_ffn),
        "gate_wt": np.ascontiguousarray(
            np.asarray(L0_ffn_gate_w).reshape(E, KD, P).transpose(2, 1, 0)).reshape(P, KD * E),
        "gate_b": np.ascontiguousarray(L0_ffn_gate_b),
        "w1t": np.ascontiguousarray(
            np.asarray(L0_ffn_w1).reshape(E, H, KD, P).transpose(0, 3, 2, 1)).reshape(E, P, KD * H),
        "b1t": np.ascontiguousarray(
            np.asarray(L0_ffn_b1).reshape(E, KH, P).transpose(2, 0, 1)).reshape(P, E * KH),
        "w2t": np.ascontiguousarray(
            np.asarray(L0_ffn_w2).reshape(E, D, KH, P).transpose(0, 3, 2, 1)).reshape(E, P, KH * D),
        "b2": np.ascontiguousarray(L0_ffn_b2).reshape(E * D),
    }
    nc = bacc.Bacc("TRN2", target_bir_lowering=False, num_devices=1)
    args = [nc.dram_tensor(f"in_{n}", a.shape, mybir.dt.from_np(a.dtype), kind="ExternalInput").ap()
            for n, a in arrays.items()]
    out = nc.dram_tensor("out_rows", (TOKENS, D), F32, kind="ExternalOutput").ap()
    gated_cross_attention_moe(nc, *args, out)
    result = run_bass_kernel_spmd(nc, [{f"in_{n}": a for n, a in arrays.items()}], core_ids=[0])
    return result.results[0]["out_rows"].reshape(B, S, D)
```

```python
from contextlib import ExitStack

import concourse.bass as bass
from concourse import mybir

P = 128
ALU = mybir.AluOpType
ACT = mybir.ActivationFunctionType
AX_X = mybir.AxisListType.X
F32 = mybir.dt.float32
BF16 = mybir.dt.bfloat16
I32 = mybir.dt.int32
U32 = mybir.dt.uint32

EPS = 1e-5
B, S, D = 8, 112, 256
CTX = 375
E, H = 8, 1024
TOKENS = B * S
KD, KH = D // P, H // P
CC, CR = 3, CTX // 3
ROW = D + 4
MEAN, VAR, RSTD, VEPS = D, D + 1, D + 2, D + 3
CHUNKS = TOKENS // P
AHEAD = 4
MAX_OVER = CHUNKS - 1
SLOTS = CHUNKS * E
SMALL = KD * E + E + E * KH + 2
LEAST = -3.4e38
NOWHERE = 65536.0


def gated_cross_attention_moe(nc, x, ctx_rows, ctx_cols, small, w1t, w2t, b2, out):
    x2_dram = nc.dram_tensor("x2_rows", (TOKENS, ROW), F32, kind="Internal").ap()
    with ExitStack() as stack:
        def sb(name, shape, dt=F32):
            return stack.enter_context(nc.sbuf_tensor(name, shape, dt))

        def ps(name, shape):
            return stack.enter_context(nc.psum_tensor(name, shape, F32))

        def sem(name):
            return stack.enter_context(nc.semaphore(name))

        w1 = sb("w1", [P, E, KD * H])
        w2 = sb("w2", [P, E, KH * D])
        b2b = sb("b2b", [P, E * D])
        smalls = sb("smalls", [P, SMALL])
        gw, gb = smalls[:, 0:KD * E], smalls[:, KD * E:(KD + 1) * E]
        b1, gates = smalls[:, (KD + 1) * E:SMALL - 2], smalls[:, SMALL - 2:SMALL]
        tg = sb("tg", [P, 2])
        region = sb("region", [P, B * (KD * CTX + CC * D)])
        cxT = region[:, 0:B * KD * CTX].rearrange("p (b n) -> p b n", b=B)
        cx = region[:, B * KD * CTX:].rearrange("p (b n) -> p b n", b=B)
        hid = region[:, 0:2 * H].rearrange("p (q n) -> p q n", q=2)
        hidT = region[:, 2 * H:3 * H].rearrange("p (k n) -> p k n", k=KH)
        xg = region[:, 3 * H:3 * H + (E + 2) * ROW].rearrange("p (j n) -> p j n", j=E + 2)
        xgn = region[:, 6 * H:6 * H + 2 * D].rearrange("p (q n) -> p q n", q=2)
        xgT = region[:, 6 * H + 2 * D:6 * H + 4 * D].rearrange("p (q n) -> p q n", q=2)

        xn = w1[:, E - 1, 0:2 * D].rearrange("p (q n) -> p q n", q=2)
        xn2 = w2[:, E - 1, 0:2 * D].rearrange("p (q n) -> p q n", q=2)
        gel = w2[:, E - 1, 2 * D:2 * D + 2 * CTX].rearrange("p (q n) -> p q n", q=2)
        gelT = w2[:, E - 1, 1280:1280 + 2 * CC * S].rearrange("p (q n) -> p q n", q=2)

        x2 = sb("x2", [P, B, ROW])
        xnT = sb("xnT", [P, 2, KD * S])
        xn2T = sb("xn2T", [P, 2, KD * S])
        pick_r0 = sb("pick_r0", [P, B, P], BF16)
        pick_e0 = sb("pick_e0", [P, B, 2, E], BF16)
        stats = sb("stats", [P, 6])
        stats2 = sb("stats2", [P, 6])
        mv = sb("mv", [P, 2, 4])
        power = sb("power", [P, 1])
        eps = sb("eps", [P, 1])

        ident = sb("ident", [P, P])
        tri = sb("tri", [P, S], BF16)
        ones = sb("ones", [P, P], BF16)
        iota_r = sb("iota_r", [P, P], BF16)
        iota_e = sb("iota_e", [P, E])
        iota_k = sb("iota_k", [P, SLOTS])
        iota_b = sb("iota_b", [P, B])
        iota_j = sb("iota_j", [P, MAX_OVER])
        row_1 = sb("row_1", [P, 1])
        upto = sb("upto", [P, E, E])

        lg = sb("lg", [P, B, E])
        cand = sb("cand", [P, B, E])
        mx = sb("mx", [P, B])
        first = sb("first", [P, B])
        oh = sb("oh", [P, B, E], BF16)
        rk = sb("rk", [P, B, E])
        rank = sb("rank", [P, B])
        rank_i = sb("rank_i", [P, B], I32)
        rmod = sb("rmod", [P, B])
        base = sb("base", [P, B], I32)
        key = sb("key", [P, B])
        pick_r = sb("pick_r", [P, B, P], BF16)
        pick_k = sb("pick_k", [P, B, 2 * SLOTS], BF16)
        id1 = sb("id1", [P, SLOTS])
        empty = sb("empty", [P, SLOTS])
        from_row0 = sb("from_row0", [P, E], U32)
        to_row0 = sb("to_row0", [P, E], U32)
        empty0 = sb("empty0", [P, E])
        from_row = sb("from_row", [P, SLOTS], U32)
        to_row = sb("to_row", [P, SLOTS], U32)
        from_over = sb("from_over", [P, 2], U32)
        to_over = sb("to_over", [P, 2], U32)
        flags = sb("flags", [P, E, MAX_OVER])
        over = sb("over", [P, E])
        cum2 = sb("cum2", [P, E, E])
        cum = sb("cum", [P, E])
        before = sb("before", [P, MAX_OVER, E])
        before_n = sb("before_n", [P, MAX_OVER, E])
        ej = sb("ej", [P, MAX_OVER])
        sj = sb("sj", [P, MAX_OVER])
        cj = sb("cj", [P, MAX_OVER])
        ctrl = sb("ctrl", [P, 2 * MAX_OVER + 1], I32)

        banks = [ps(f"bank{i}", [P, 512]) for i in range(8)]
        xnT_ps, sc_ps, gelT_ps, at_ps, xn2T_ps, cnt_ps, lg_ps, rk_ps = banks
        tok0_ps, rk7_ps = banks[0], banks[1]
        tok_ps = banks[7]
        h_ps = banks[0:2]
        hT_ps = banks[2:6]
        y_ps, xgT_ps = banks[6], banks[7]

        x_in = [sem("x_in0"), sem("x_in1"), sem("x_in2")]
        small_in, b2_in = sem("small_in"), sem("b2_in")
        ctx_in = [sem("ctx_in0"), sem("ctx_in1")]
        w1_in = [sem("w1_in0"), sem("w1_in1")]
        w2_in = [sem("w2_in0"), sem("w2_in1")]
        pool_step = sem("pool_step")
        ident_ok, consts_ok = sem("ident_ok"), sem("consts_ok")
        tg_ok, veps_ok = sem("tg_ok"), sem("veps_ok")
        s1_ok, stats_ok, rstd_ok, xn_ok = sem("s1_ok"), sem("stats_ok"), sem("rstd_ok"), sem("xn_ok")
        xnT_done, xnT_ok = sem("xnT_done"), sem("xnT_ok")
        sc_done, gel_ok = sem("sc_done"), sem("gel_ok")
        gelT_done, gelT_ok = sem("gelT_done"), sem("gelT_ok")
        at_done, x2_ok = sem("at_done"), sem("x2_ok")
        s2_ok, stats2_ok, rstd2_ok, xn2_ok = sem("s2_ok"), sem("stats2_ok"), sem("rstd2_ok"), sem("xn2_ok")
        xn2T_done, xn2T_ok, lg_done = sem("xn2T_done"), sem("xn2T_ok"), sem("lg_done")
        x2_stored = sem("x2_stored")
        dve_step = sem("dve_step")
        route_step, oh_ok, picks0_ok = sem("route_step"), sem("oh_ok"), sem("picks0_ok")
        rk_done, rk7_done, rank_read = sem("rk_done"), sem("rk7_done"), sem("rank_read")
        tok0_done, rows0_ok, to_rows0_ok = sem("tok0_done"), sem("rows0_ok"), sem("to_rows0_ok")
        picks_ok, tok_done, tok_read = sem("picks_ok"), sem("tok_done"), sem("tok_read")
        rows_ok, ctrl_ok = sem("rows_ok"), sem("ctrl_ok")
        cnt_done, cnt_read = sem("cnt_done"), sem("cnt_read")
        xg_in = [sem("xg_in0"), sem("xg_in1")]
        over_in = [sem("over_in0"), sem("over_in1")]
        over_idx = sem("over_idx")
        xgn_ok, xgT_done, xgT_ok = sem("xgn_ok"), sem("xgT_done"), sem("xgT_ok")
        h_done = sem("h_done")
        h0_ok, h1_ok = sem("h0_ok"), sem("h1_ok")
        hT_done = sem("hT_done")
        hTa_ok, hTd_ok = sem("hTa_ok"), sem("hTd_ok")
        y_done, base_ok, o_ok = sem("y_done"), sem("base_ok"), sem("o_ok")
        out_done = [sem("out_done0"), sem("out_done1")]

        block = stack.enter_context(nc.Block())

        @block.sync
        def _(sp):
            def load_context(b, q):
                sp.dma_start(cxT[:, b, :], ctx_cols[b]).then_inc(ctx_in[q], 16)
                sp.dma_start(cx[0:CR, b, :].rearrange("p (c d) -> p c d", c=CC),
                             ctx_rows[b].rearrange("(c p) d -> p c d", p=CR)).then_inc(ctx_in[q], 16)

            def load_expert(e, q):
                sp.dma_start(w1[:, e, :], w1t[e]).then_inc(w1_in[q], 16)
                sp.dma_start(w2[:, e, :], w2t[e]).then_inc(w2_in[q], 16)

            sp.dma_start(x2[0:S, 0, 0:D], x[0:S]).then_inc(x_in[0], 16)
            for b in range(2):
                load_context(b, b)
            with sp.Fori(1, B // 2) as t:
                for q in range(2):
                    sp.wait_ge(ctx_in[q], 32 * t)
                    load_context(2 * t + q, q)
            for e in range(2):
                load_expert(e, e)
            for q in range(2):
                sp.wait_ge(xg_in[q], 16)
            sp.dma_start(b2b[:], b2.partition_broadcast(P)).then_inc(b2_in, 16)
            with sp.Fori(1, E // 2) as t:
                for q in range(2):
                    sp.wait_ge(w1_in[q], 16 * t)
                    sp.wait_ge(w2_in[q], 16 * t)
                    load_expert(2 * t + q, q)

        @block.gpsimd
        def _(pool):
            pool.memset(ident[:], 0.0).then_inc(pool_step, 1)
            pool.wait_ge(pool_step, 1)
            pool.affine_select(out=ident[:], in_=ident[:], compare_op=ALU.not_equal, fill=1.0, base=0,
                               pattern=[[-1, P]], channel_multiplier=1).then_inc(ident_ok, 1)
            pool.memset(power[:], -0.5).then_inc(pool_step, 1)
            pool.memset(eps[:], EPS).then_inc(pool_step, 1)
            pool.memset(ones[:], 1.0).then_inc(pool_step, 1)
            pool.wait_ge(pool_step, 4)
            pool.affine_select(out=tri[:], in_=ones[:, 0:S], compare_op=ALU.is_gt, fill=0.0, base=0,
                               pattern=[[1, S]], channel_multiplier=-1).then_inc(consts_ok, 1)
            pool.iota(iota_r[:], [[1, P]], base=0, channel_multiplier=0,
                      allow_small_or_imprecise_dtypes=True).then_inc(consts_ok, 1)
            pool.iota(iota_e[:], [[-1, E]], base=E, channel_multiplier=0,
                      allow_small_or_imprecise_dtypes=True).then_inc(consts_ok, 1)
            pool.iota(iota_k[:], [[P, SLOTS]], base=-P * E, channel_multiplier=0,
                      allow_small_or_imprecise_dtypes=True).then_inc(consts_ok, 1)
            pool.iota(iota_b[:], [[1, B]], base=0, channel_multiplier=0,
                      allow_small_or_imprecise_dtypes=True).then_inc(consts_ok, 1)
            pool.iota(iota_j[:], [[1, MAX_OVER]], base=0, channel_multiplier=0,
                      allow_small_or_imprecise_dtypes=True).then_inc(consts_ok, 1)
            pool.iota(row_1[:], [[0, 1]], base=1, channel_multiplier=1,
                      allow_small_or_imprecise_dtypes=True).then_inc(consts_ok, 1)
            pool.memset(upto[:], 1.0).then_inc(pool_step, 1)
            pool.wait_ge(pool_step, 5)
            pool.affine_select(out=upto[:], in_=upto[:], compare_op=ALU.is_ge, fill=0.0, base=0,
                               pattern=[[1, E], [-1, E]], channel_multiplier=0).then_inc(consts_ok, 1)
            veps = [0]

            def inverse_std(v):
                pool.tensor_tensor(v[:, 3:4], v[:, 1:2], eps[0:S, :], ALU.add).then_inc(veps_ok, 1)
                veps[0] += 1
                pool.wait_ge(veps_ok, veps[0])
                return pool.tensor_tensor(v[:, 2:3], v[:, 3:4], power[0:S, :], ALU.pow)

            def of_x(b):
                pool.wait_ge(stats_ok, b + 1)
                inverse_std(mv[0:S, b % 2, :]).then_inc(rstd_ok, 1)

            for b in range(AHEAD):
                of_x(b)
            for b in range(B):
                pool.wait_ge(stats2_ok, b + 1)
                inverse_std(x2[0:S, b, MEAN:]).then_inc(rstd2_ok, 1)
                if b + AHEAD < B:
                    of_x(b + AHEAD)

            def gather(to, idx):
                return pool.indirect_dma_start(
                    out=to, out_offset=None, in_=x2_dram, in_offset=bass.IndirectOffsetOnAxis(ap=idx, axis=0),
                    bounds_check=TOKENS - 1, oob_is_err=False)

            def scatter(rows, idx):
                return pool.indirect_dma_start(
                    out=out, out_offset=bass.IndirectOffsetOnAxis(ap=idx, axis=0), in_=rows, in_offset=None,
                    bounds_check=TOKENS - 1, oob_is_err=False)

            pool.wait_ge(x2_stored, 16 * B)
            pool.wait_ge(rows0_ok, 1)
            for e in range(E):
                if e >= 2:
                    pool.wait_ge(xg_in[e % 2], 16 * (e // 2))
                gather(xg[:, e, :], from_row0[:, e:e + 1]).then_inc(xg_in[e % 2], 16)

            pool.wait_ge(ctrl_ok, 1)
            pool.wait_ge(rows_ok, 1)
            n_over = pool.value_load(ctrl[0:1, 2 * MAX_OVER:2 * MAX_OVER + 1], min_val=0, max_val=MAX_OVER)

            def over_gather(m):
                q = m % 2
                col = pool.value_load(ctrl[0:1, MAX_OVER + m:MAX_OVER + m + 1], min_val=0, max_val=SLOTS - 1)
                pool.tensor_copy(from_over[:, q:q + 1], from_row[:, bass.ds(col, 1)]).then_inc(over_idx, 1)
                pool.tensor_copy(to_over[:, q:q + 1], to_row[:, bass.ds(col, 1)]).then_inc(over_idx, 1)
                pool.wait_ge(over_idx, 2 * (m + 1))
                gather(xg[:, E + q, :], from_over[:, q:q + 1]).then_inc(over_in[q], 16)

            for m in range(2):
                with pool.If(n_over > m):
                    over_gather(m)
            pool.wait_ge(to_rows0_ok, 1)
            for e in range(E):
                pool.wait_ge(o_ok, e + 1)
                scatter(xg[:, e, 0:D], to_row0[:, e:e + 1]).then_inc(out_done[0], 16)
            for m in range(MAX_OVER):
                with pool.If(n_over > m):
                    pool.wait_ge(o_ok, E + 1 + m)
                    scatter(xg[:, E + m % 2, 0:D], to_over[:, m % 2:m % 2 + 1]).then_inc(out_done[1], 16)
                    pool.wait_ge(out_done[1], 16 * (m + 1))
                if m + 2 < MAX_OVER:
                    with pool.If(n_over > m + 2):
                        over_gather(m + 2)
            pool.wait_ge(out_done[0], 16 * E)

        @block.scalar
        def _(act):
            act.dma_start(smalls[:], small).then_inc(small_in, 16)
            act.dma_start(x2[0:S, 1:2, 0:D],
                          x[S:2 * S].rearrange("(b p) d -> p b d", p=S)).then_inc(x_in[1], 16)
            act.dma_start(x2[0:S, 2:B, 0:D],
                          x[2 * S:TOKENS].rearrange("(b p) d -> p b d", p=S)).then_inc(x_in[2], 16)
            act.wait_ge(small_in, 16)
            act.activation(tg[:], gates, ACT.Tanh).then_inc(tg_ok, 1)

            def xnT_copy(b):
                act.wait_ge(xnT_done, b + 1)
                act.activation(xnT[:, b % 2, :], xnT_ps[:, 0:KD * S], ACT.Copy).then_inc(xnT_ok, 1)

            def gelu(b):
                act.wait_ge(sc_done, b + 1)
                act.activation(gel[0:S, b % 2, 0:CTX], sc_ps[0:S, 0:CTX], ACT.Gelu_apprx_tanh).then_inc(gel_ok, 1)

            def gelT_copy(b):
                act.wait_ge(gelT_done, b + 1)
                act.activation(gelT[0:CR, b % 2, :], gelT_ps[0:CR, 0:CC * S], ACT.Copy).then_inc(gelT_ok, 1)

            def xn2T_copy(b):
                act.wait_ge(rstd2_ok, b + 1)
                act.dma_start(x2_dram[b * S:(b + 1) * S, :], x2[0:S, b, :]).then_inc(x2_stored, 16)
                act.wait_ge(xn2T_done, b + 1)
                act.activation(xn2T[:, b % 2, :], xn2T_ps[:, 0:KD * S], ACT.Copy).then_inc(xn2T_ok, 1)

            xnT_copy(0)
            gelu(0)
            xnT_copy(1)
            for b in range(B):
                gelT_copy(b)
                if b + 1 < B:
                    gelu(b + 1)
                if b + 2 < B:
                    xnT_copy(b + 2)
                if b >= 1:
                    xn2T_copy(b - 1)
            xn2T_copy(B - 1)

            def xgT_copy(j, q):
                act.wait_ge(xgT_done, j + 1)
                act.activation(xgT[:, q, :], xgT_ps[:, 0:D], ACT.Copy).then_inc(xgT_ok, 1)

            def h0_copy(j, q):
                act.wait_ge(h_done, 2 * j + 1)
                act.activation(hid[:, q, 0:H // 2], h_ps[0][:], ACT.Copy).then_inc(h0_ok, 1)

            def relu(j, e):
                for k in (0, 2):
                    act.wait_ge(hT_done, 4 * j + k + 1)
                    for r in range(2):
                        act.activation(hidT[:, 2 * k + r, :], hT_ps[k][:, r * P:(r + 1) * P], ACT.Relu,
                                       bias=b1[:, bass.ds(e * KH + 2 * k + r, 1)]).then_inc(hTa_ok, 1)

            xgT_copy(0, 0)
            h0_copy(0, 0)
            xgT_copy(1, 1)
            with act.Fori(0, E // 2 - 1) as t:
                for q in range(2):
                    j = 2 * t + q
                    h0_copy(j + 1, 1 - q)
                    xgT_copy(j + 2, q)
                    relu(j, j)
            act.wait_ge(ctrl_ok, 1)
            n_over = act.value_load(ctrl[0:1, 2 * MAX_OVER:2 * MAX_OVER + 1], min_val=0, max_val=MAX_OVER)
            h0_copy(E - 1, 1)
            with act.If(n_over > 0):
                xgT_copy(E, 0)
            relu(E - 2, E - 2)
            with act.If(n_over > 0):
                h0_copy(E, 0)
            relu(E - 1, E - 1)
            with act.Fori(0, MAX_OVER // 2) as t:
                for q in range(2):
                    m = 2 * t + q
                    with act.If(n_over > m):
                        with act.If(n_over > m + 1):
                            xgT_copy(E + m + 1, 1 - q)
                            h0_copy(E + m + 1, 1 - q)
                        e = act.value_load(ctrl[0:1, bass.ds(m, 1)], min_val=0, max_val=E - 1)
                        relu(E + m, e)

        @block.vector
        def _(dve):
            def stats_x(b):
                dve.wait_ge(x_in[min(b, 2)], 16)
                if b >= 2:
                    dve.wait_ge(xn_ok, b - 1)
                dve.bn_stats(stats[0:S, :], x2[0:S, b, 0:D]).then_inc(s1_ok, 1)
                dve.wait_ge(s1_ok, b + 1)
                dve.bn_aggr(mv[0:S, b % 2, 0:2], stats[0:S, :]).then_inc(stats_ok, 1)

            def norm_x(b):
                if b >= 2:
                    dve.wait_ge(xnT_done, b - 1)
                dve.wait_ge(rstd_ok, b + 1)
                dve.tensor_scalar(xn[0:S, b % 2, :], x2[0:S, b, 0:D], mv[0:S, b % 2, 0:1], mv[0:S, b % 2, 2:3],
                                  ALU.subtract, ALU.mult).then_inc(xn_ok, 1)

            def residual(b):
                dve.wait_ge(at_done, b + 1)
                dve.scalar_tensor_tensor(out=x2[0:S, b, 0:D], in0=at_ps[0:S, 0:D], scalar=tg[0:S, 0:1],
                                         in1=x2[0:S, b, 0:D], op0=ALU.mult, op1=ALU.add).then_inc(x2_ok, 1)
                dve.wait_ge(x2_ok, b + 1)
                dve.bn_stats(stats2[0:S, :], x2[0:S, b, 0:D]).then_inc(s2_ok, 1)
                dve.wait_ge(s2_ok, b + 1)
                dve.bn_aggr(x2[0:S, b, MEAN:MEAN + 2], stats2[0:S, :]).then_inc(stats2_ok, 1)

            def norm_x2(b):
                if b >= 2:
                    dve.wait_ge(xn2T_done, b - 1)
                dve.wait_ge(rstd2_ok, b + 1)
                dve.tensor_scalar(xn2[0:S, b % 2, :], x2[0:S, b, 0:D], x2[0:S, b, MEAN:MEAN + 1],
                                  x2[0:S, b, RSTD:RSTD + 1], ALU.subtract, ALU.mult).then_inc(xn2_ok, 1)

            routed = [0]

            def link(instruction):
                instruction.then_inc(route_step, 1)
                routed[0] += 1
                dve.wait_ge(route_step, routed[0])

            def route(b):
                dve.wait_ge(lg_done, b + 1)
                link(dve.tensor_tensor_reduce(out=lg[0:S, b, :], in0=lg_ps[0:S, b * E:(b + 1) * E], in1=gb[0:S, :],
                                              scale=1.0, scalar=LEAST, op0=ALU.add, op1=ALU.max,
                                              accum_out=mx[0:S, b:b + 1]))
                link(dve.scalar_tensor_tensor(out=cand[0:S, b, :], in0=lg[0:S, b, :], scalar=mx[0:S, b:b + 1],
                                              in1=iota_e[0:S, :], op0=ALU.is_equal, op1=ALU.mult))
                link(dve.tensor_reduce(first[0:S, b:b + 1], cand[0:S, b, :], AX_X, ALU.max))
                dve.tensor_scalar(oh[0:S, b, :], iota_e[0:S, :], first[0:S, b:b + 1], None,
                                  ALU.is_equal).then_inc(oh_ok, 1)
                dve.tensor_scalar(pick_e0[0:S, b, 0, :], iota_e[0:S, :], first[0:S, b:b + 1], row_1[0:S, 0:1],
                                  ALU.is_equal, ALU.mult)
                dve.tensor_scalar(pick_e0[0:S, b, 1, :], iota_e[0:S, :], first[0:S, b:b + 1], float(S * b),
                                  ALU.is_equal, ALU.mult)

            for b in range(AHEAD):
                stats_x(b)
                norm_x(b)
            dve.wait_ge(tg_ok, 1)
            dve.wait_ge(consts_ok, 8)
            for b in range(B):
                if b >= 2:
                    route(b - 2)
                residual(b)
                if b + AHEAD < B:
                    stats_x(b + AHEAD)
                if b == B - 1:
                    route(b - 1)
                norm_x2(b)
                if b + AHEAD < B:
                    norm_x(b + AHEAD)

            L = B - 1
            dve.wait_ge(rk_done, 1)
            link(dve.tensor_tensor(rk[0:S, 0:L], rk_ps[0:S, 0:L * E].rearrange("p (b e) -> p b e", b=L),
                                   oh[0:S, 0:L], ALU.mult))
            link(dve.tensor_reduce(rank[0:S, 0:L], rk[0:S, 0:L], AX_X, ALU.add))
            for b in range(L):
                last = dve.tensor_scalar(pick_r0[0:S, b, :], iota_r[0:S, :], rank[0:S, b:b + 1], None, ALU.is_equal)
            last.then_inc(picks0_ok, 1)
            route(L)
            dve.wait_ge(oh_ok, B)
            dve.wait_ge(rk7_done, 1)
            link(dve.tensor_tensor_reduce(out=rk[0:S, L, :], in0=rk7_ps[0:S, 0:E], in1=oh[0:S, L, :],
                                          scale=1.0, scalar=0.0, op0=ALU.mult, op1=ALU.add,
                                          accum_out=rank[0:S, L:B]))
            dve.tensor_scalar(pick_r0[0:S, L, :], iota_r[0:S, :], rank[0:S, L:B], None,
                              ALU.is_equal).then_inc(picks0_ok, 1)
            dve.wait_ge(tok0_done, 1)
            dve.tensor_scalar(from_row0[:], tok0_ps[:, 0:E], -1.0, 0.0, ALU.add, ALU.max).then_inc(rows0_ok, 1)
            link(dve.tensor_scalar(empty0[:], tok0_ps[:, 0:E], 0.0, NOWHERE, ALU.is_equal, ALU.mult))
            dve.scalar_tensor_tensor(out=to_row0[:], in0=tok0_ps[:, 0:E], scalar=-1.0, in1=empty0[:], op0=ALU.add,
                                     op1=ALU.add).then_inc(to_rows0_ok, 1)

            steps = [0]

            def step(instruction):
                instruction.then_inc(dve_step, 1)
                steps[0] += 1
                dve.wait_ge(dve_step, steps[0])

            dve.wait_ge(cnt_done, 1)
            for c in range(MAX_OVER):
                last = dve.tensor_scalar(flags[:, :, c], cnt_ps[:, 0:E], float(P * (c + 1)), None, ALU.is_gt)
            last.then_inc(cnt_read, 1)
            dve.wait_ge(cnt_read, 1)
            step(dve.tensor_reduce(over[:], flags[:], AX_X, ALU.add))
            step(dve.tensor_tensor(cum2[:], upto[:], over[:].unsqueeze(1).to_broadcast([P, E, E]), ALU.mult))
            step(dve.tensor_reduce(cum[:], cum2[:], AX_X, ALU.add))
            step(dve.tensor_tensor(before[:], cum[:].unsqueeze(1).to_broadcast([P, MAX_OVER, E]),
                                   iota_j[:].unsqueeze(2).to_broadcast([P, MAX_OVER, E]), ALU.is_le))
            step(dve.tensor_reduce(ej[:], before[:], AX_X, ALU.add))
            step(dve.tensor_tensor(before_n[:], before[:], over[:].unsqueeze(1).to_broadcast([P, MAX_OVER, E]),
                                   ALU.mult))
            step(dve.tensor_reduce(sj[:], before_n[:], AX_X, ALU.add))
            step(dve.scalar_tensor_tensor(out=cj[:], in0=iota_j[:], scalar=1.0, in1=sj[:], op0=ALU.add,
                                          op1=ALU.subtract))
            step(dve.tensor_copy(ctrl[:, 0:MAX_OVER], ej[:]))
            step(dve.scalar_tensor_tensor(out=ctrl[:, MAX_OVER:2 * MAX_OVER], in0=cj[:], scalar=float(E), in1=ej[:],
                                          op0=ALU.mult, op1=ALU.add))
            dve.tensor_copy(ctrl[:, 2 * MAX_OVER:2 * MAX_OVER + 1], cum[:, E - 1:E]).then_inc(ctrl_ok, 1)

            def over_picks():
                step(dve.tensor_copy(rank_i[0:S], rank[0:S]))
                step(dve.tensor_scalar(base[0:S], rank_i[0:S], 7, 7, ALU.arith_shift_right, ALU.logical_shift_left))
                dve.tensor_tensor(rmod[0:S], rank[0:S], base[0:S], ALU.subtract)
                step(dve.tensor_scalar(key[0:S], base[0:S], float(E), None, ALU.mult))
                step(dve.scalar_tensor_tensor(out=key[0:S], in0=first[0:S], scalar=-float(P), in1=key[0:S],
                                              op0=ALU.mult, op1=ALU.add))
                for b in range(B):
                    dve.tensor_scalar(pick_r[0:S, b, :], iota_r[0:S, :], rmod[0:S, b:b + 1], None, ALU.is_equal)
                step(dve.tensor_tensor(pick_k[0:S, :, 0:SLOTS],
                                       iota_k[0:S, :].unsqueeze(1).to_broadcast([S, B, SLOTS]),
                                       key[0:S, :].unsqueeze(2).to_broadcast([S, B, SLOTS]), ALU.is_equal))
                step(dve.tensor_tensor(pick_k[0:S, :, SLOTS:2 * SLOTS], pick_k[0:S, :, 0:SLOTS],
                                       iota_b[0:S, :].unsqueeze(2).to_broadcast([S, B, SLOTS]), ALU.mult))
                dve.tensor_scalar(pick_k[0:S, :, 0:SLOTS], pick_k[0:S, :, 0:SLOTS], row_1[0:S, 0:1], None,
                                  ALU.mult).then_inc(picks_ok, 1)

            def over_table():
                dve.wait_ge(tok_done, 1)
                step(dve.tensor_copy(id1[:], tok_ps[:, 0:SLOTS]))
                dve.scalar_tensor_tensor(out=id1[:], in0=tok_ps[:, SLOTS:2 * SLOTS], scalar=float(S), in1=id1[:],
                                         op0=ALU.mult, op1=ALU.add).then_inc(tok_read, 1)
                dve.wait_ge(tok_read, 1)
                dve.tensor_scalar(from_row[:], id1[:], -1.0, 0.0, ALU.add, ALU.max)
                step(dve.tensor_scalar(empty[:], id1[:], 0.0, NOWHERE, ALU.is_equal, ALU.mult))
                dve.scalar_tensor_tensor(out=to_row[:], in0=id1[:], scalar=-1.0, in1=empty[:], op0=ALU.add,
                                         op1=ALU.add).then_inc(rows_ok, 1)

            def norm_block(j, q, rows):
                dve.tensor_scalar(xgn[:, q, :], rows[:, 0:D], rows[:, MEAN:MEAN + 1], rows[:, RSTD:RSTD + 1],
                                  ALU.subtract, ALU.mult).then_inc(xgn_ok, 1)

            def h1_copy(j, q):
                dve.wait_ge(h_done, 2 * j + 2)
                dve.tensor_copy(hid[:, q, H // 2:H], h_ps[1][:]).then_inc(h1_ok, 1)

            def relu(j, e):
                for k in (1, 3):
                    dve.wait_ge(hT_done, 4 * j + k + 1)
                    for r in range(2):
                        dve.tensor_scalar(hidT[:, 2 * k + r, :], hT_ps[k][:, r * P:(r + 1) * P],
                                          b1[:, bass.ds(e * KH + 2 * k + r, 1)], 0.0, ALU.add,
                                          ALU.max).then_inc(hTd_ok, 1)

            def bias_2(e, rows):
                dve.scalar_tensor_tensor(out=rows[:, 0:D], in0=b2b[:, bass.ds(e * D, D)], scalar=tg[:, 1:2],
                                         in1=rows[:, 0:D], op0=ALU.mult, op1=ALU.add).then_inc(base_ok, 1)

            def finish(j, rows):
                dve.wait_ge(base_ok, j + 1)
                dve.wait_ge(y_done, j + 1)
                dve.scalar_tensor_tensor(out=rows[:, 0:D], in0=y_ps[:, 0:D], scalar=tg[:, 1:2], in1=rows[:, 0:D],
                                         op0=ALU.mult, op1=ALU.add).then_inc(o_ok, 1)

            for j in range(2):
                dve.wait_ge(xg_in[j], 16)
                norm_block(j, j, xg[:, j, :])
            h1_copy(0, 0)
            over_picks()
            for j in range(2):
                dve.wait_ge(xg_in[j], 32)
                dve.wait_ge(xgT_done, j + 1)
                norm_block(j + 2, j, xg[:, j + 2, :])
                h1_copy(j + 1, 1 - j)
                relu(j, j)
                dve.wait_ge(b2_in, 16)
                dve.wait_ge(xgn_ok, j + 1)
                bias_2(j, xg[:, j, :])
                finish(j, xg[:, j, :])
                if j == 0:
                    over_table()
            with dve.Fori(1, E // 2 - 1) as t:
                for q in range(2):
                    j = 2 * t + q
                    dve.wait_ge(xg_in[q], 16 * (t + 2))
                    dve.wait_ge(xgT_done, j + 1)
                    norm_block(j + 2, q, xg[:, j + 2, :])
                    h1_copy(j + 1, 1 - q)
                    relu(j, j)
                    bias_2(j, xg[:, j, :])
                    finish(j, xg[:, j, :])
            n_over = dve.value_load(ctrl[0:1, 2 * MAX_OVER:2 * MAX_OVER + 1], min_val=0, max_val=MAX_OVER)
            with dve.If(n_over > 0):
                dve.wait_ge(over_in[0], 16)
                dve.wait_ge(xgT_done, E - 1)
                norm_block(E, 0, xg[:, E, :])
            h1_copy(E - 1, 1)
            relu(E - 2, E - 2)
            bias_2(E - 2, xg[:, E - 2, :])
            finish(E - 2, xg[:, E - 2, :])
            with dve.If(n_over > 0):
                h1_copy(E, 0)
            relu(E - 1, E - 1)
            bias_2(E - 1, xg[:, E - 1, :])
            finish(E - 1, xg[:, E - 1, :])
            with dve.Fori(0, MAX_OVER // 2) as t:
                for q in range(2):
                    m = 2 * t + q
                    with dve.If(n_over > m):
                        with dve.If(n_over > m + 1):
                            dve.wait_ge(over_in[1 - q], 16 * (t + q + 1))
                            dve.wait_ge(xgT_done, E + m)
                            norm_block(E + m + 1, 1 - q, xg[:, E + 1 - q, :])
                            h1_copy(E + m + 1, 1 - q)
                        e = dve.value_load(ctrl[0:1, bass.ds(m, 1)], min_val=0, max_val=E - 1)
                        relu(E + m, e)
                        bias_2(e, xg[:, E + q, :])
                        finish(E + m, xg[:, E + q, :])

        @block.tensor
        def _(pe):
            def turn_xn(b):
                pe.wait_ge(xn_ok, b + 1)
                for k in range(KD):
                    mm = pe.transpose(xnT_ps[:, k * S:(k + 1) * S], xn[0:S, b % 2, k * P:(k + 1) * P], ident[0:S, 0:S])
                mm.then_inc(xnT_done, 1)

            def scores(b):
                pe.wait_ge(xnT_ok, b + 1)
                pe.wait_ge(ctx_in[b % 2], 32 * (b // 2 + 1))
                for k in range(KD):
                    mm = pe.matmul(sc_ps[0:S, 0:CTX], xnT[:, b % 2, k * S:(k + 1) * S],
                                   cxT[:, b, k * CTX:(k + 1) * CTX], start=(k == 0), stop=(k == KD - 1))
                mm.then_inc(sc_done, 1)

            def turn_gelu(b):
                pe.wait_ge(gel_ok, b + 1)
                for c in range(CC):
                    mm = pe.transpose(gelT_ps[0:CR, c * S:(c + 1) * S], gel[0:S, b % 2, c * CR:(c + 1) * CR],
                                      ident[0:S, 0:S])
                mm.then_inc(gelT_done, 1)

            def attend(b):
                pe.wait_ge(gelT_ok, b + 1)
                if b >= 1:
                    pe.wait_ge(x2_ok, b)
                for c in range(CC):
                    mm = pe.matmul(at_ps[0:S, 0:D], gelT[0:CR, b % 2, c * S:(c + 1) * S],
                                   cx[0:CR, b, c * D:(c + 1) * D], start=(c == 0), stop=(c == CC - 1))
                mm.then_inc(at_done, 1)

            def turn_xn2(b):
                pe.wait_ge(xn2_ok, b + 1)
                if b >= 1:
                    pe.wait_ge(xn2T_ok, b)
                for k in range(KD):
                    mm = pe.transpose(xn2T_ps[:, k * S:(k + 1) * S], xn2[0:S, b % 2, k * P:(k + 1) * P],
                                      ident[0:S, 0:S])
                mm.then_inc(xn2T_done, 1)

            def logits(b):
                pe.wait_ge(xn2T_ok, b + 1)
                if b >= 1:
                    pe.wait_ge(oh_ok, b)
                for k in range(KD):
                    mm = pe.matmul(lg_ps[0:S, b * E:(b + 1) * E], xn2T[:, b % 2, k * S:(k + 1) * S],
                                   gw[:, k * E:(k + 1) * E], start=(k == 0), stop=(k == KD - 1))
                mm.then_inc(lg_done, 1)

            pe.wait_ge(ident_ok, 1)
            pe.wait_ge(small_in, 16)
            turn_xn(0)
            scores(0)
            turn_xn(1)
            for b in range(B):
                turn_gelu(b)
                if b >= 2:
                    logits(b - 2)
                if b + 1 < B:
                    scores(b + 1)
                if b + 2 < B:
                    turn_xn(b + 2)
                attend(b)
                if b >= 1:
                    turn_xn2(b - 1)
            logits(B - 2)
            turn_xn2(B - 1)

            L = B - 1
            flat = oh[0:S].rearrange("p b e -> p (b e)")
            pe.wait_ge(consts_ok, 8)
            pe.wait_ge(oh_ok, L)
            pe.matmul(rk_ps[0:S, 0:L * E], tri[0:S, :], flat[:, 0:L * E], start=True, stop=False)
            for s in range(1, L):
                mm = pe.matmul(rk_ps[0:S, s * E:L * E], ones[0:S, 0:S], flat[:, 0:(L - s) * E], start=False,
                               stop=(s == L - 1))
            mm.then_inc(rk_done, 1)
            logits(L)
            for b in range(L):
                pe.matmul(rk7_ps[0:S, 0:E], ones[0:S, 0:S], oh[0:S, b, :], start=(b == 0), stop=False)

            def tokens(b):
                for n in range(2):
                    mm = pe.matmul(tok0_ps[:, 0:E], pick_r0[0:S, b, :], pick_e0[0:S, b, n, :],
                                   start=(b == 0 and n == 0), stop=(b == L and n == 1))
                return mm

            pe.wait_ge(picks0_ok, 1)
            for b in range(L):
                tokens(b)
            pe.wait_ge(oh_ok, B)
            pe.matmul(rk7_ps[0:S, 0:E], tri[0:S, :], oh[0:S, L, :], start=False, stop=True).then_inc(rk7_done, 1)
            for b in range(B):
                mm = pe.matmul(cnt_ps[:, 0:E], ones[0:S, :], oh[0:S, b, :], start=(b == 0), stop=(b == B - 1))
            mm.then_inc(cnt_done, 1)
            pe.wait_ge(picks0_ok, 2)
            tokens(L).then_inc(tok0_done, 1)

            def turn_block(j, q):
                pe.wait_ge(xgn_ok, j + 1)
                for k in range(KD):
                    mm = pe.transpose(xgT_ps[:, k * P:(k + 1) * P], xgn[:, q, k * P:(k + 1) * P], ident[:])
                mm.then_inc(xgT_done, 1)

            def up(j, q, e, later=True):
                pe.wait_ge(xgT_ok, j + 1)
                for n, read in enumerate((h0_ok, h1_ok)):
                    if later:
                        pe.wait_ge(read, j)
                    for k in range(KD):
                        mm = pe.matmul(h_ps[n][:], xgT[:, q, k * P:(k + 1) * P],
                                       w1[:, e, k * H + n * 512:k * H + (n + 1) * 512],
                                       start=(k == 0), stop=(k == KD - 1))
                    mm.then_inc(h_done, 1)

            def turn_hidden(j, q):
                pe.wait_ge(h0_ok, j + 1)
                pe.wait_ge(h1_ok, j + 1)
                for k in range(KH // 2):
                    for r in range(2):
                        mm = pe.transpose(hT_ps[k][:, r * P:(r + 1) * P],
                                          hid[:, q, (2 * k + r) * P:(2 * k + r + 1) * P], ident[:])
                    mm.then_inc(hT_done, 1)

            def down(j, q, e, later=True):
                if later:
                    pe.wait_ge(o_ok, j)
                for part in range(KH):
                    pe.wait_ge((hTa_ok, hTd_ok)[part // 2 % 2], 4 * j + part // 4 * 2 + part % 2 + 1)
                    mm = pe.matmul(y_ps[:, 0:D], hidT[:, part, :], w2[:, e, part * D:(part + 1) * D],
                                   start=(part == 0), stop=(part == KH - 1))
                mm.then_inc(y_done, 1)

            turn_block(0, 0)
            pe.wait_ge(to_rows0_ok, 1)
            pe.wait_ge(w1_in[0], 16)
            up(0, 0, 0, later=False)
            turn_block(1, 1)
            for j in range(2):
                pe.wait_ge(w1_in[1 - j], 16 * (1 + j))
                up(j + 1, 1 - j, j + 1)
                if j == 1:
                    pe.wait_ge(tok_read, 1)
                turn_block(j + 2, j)
                if j == 0:
                    pe.wait_ge(cnt_read, 1)
                turn_hidden(j, j)
                pe.wait_ge(w2_in[j], 16)
                down(j, j, j, later=(j > 0))
                if j == 0:
                    pe.wait_ge(picks_ok, 1)
                    pe.wait_ge(xgT_ok, 3)
                    for b in range(B):
                        mm = pe.matmul(tok_ps[:, 0:2 * SLOTS], pick_r[0:S, b, :], pick_k[0:S, b, :],
                                       start=(b == 0), stop=(b == B - 1))
                    mm.then_inc(tok_done, 1)
            with pe.Fori(1, E // 2 - 1) as t:
                for q in range(2):
                    j = 2 * t + q
                    pe.wait_ge(w1_in[1 - q], 16 * (t + 1 + q))
                    up(j + 1, 1 - q, j + 1)
                    turn_block(j + 2, q)
                    turn_hidden(j, q)
                    pe.wait_ge(w2_in[q], 16 * (t + 1))
                    down(j, q, j)
            n_over = pe.value_load(ctrl[0:1, 2 * MAX_OVER:2 * MAX_OVER + 1], min_val=0, max_val=MAX_OVER)
            pe.wait_ge(w1_in[1], 16 * E // 2)
            up(E - 1, 1, E - 1)
            with pe.If(n_over > 0):
                turn_block(E, 0)
            turn_hidden(E - 2, 0)
            pe.wait_ge(w2_in[0], 16 * E // 2)
            down(E - 2, 0, E - 2)
            with pe.If(n_over > 0):
                up(E, 0, pe.value_load(ctrl[0:1, 0:1], min_val=0, max_val=E - 1))
            turn_hidden(E - 1, 1)
            pe.wait_ge(w2_in[1], 16 * E // 2)
            down(E - 1, 1, E - 1)
            with pe.Fori(0, MAX_OVER // 2) as t:
                for q in range(2):
                    m = 2 * t + q
                    with pe.If(n_over > m):
                        with pe.If(n_over > m + 1):
                            turn_block(E + m + 1, 1 - q)
                            up(E + m + 1, 1 - q, pe.value_load(ctrl[0:1, bass.ds(m + 1, 1)], min_val=0, max_val=E - 1))
                        e = pe.value_load(ctrl[0:1, bass.ds(m, 1)], min_val=0, max_val=E - 1)
                        turn_hidden(E + m, q)
                        down(E + m, q, e)


def kernel(x, ctx_1024, g_xattn, g_ffn, L0_ffn_gate_w, L0_ffn_gate_b, L0_ffn_w1, L0_ffn_b1, L0_ffn_w2, L0_ffn_b2):
    import numpy as np
    import concourse.bacc as bacc
    from concourse.bass_utils import run_bass_kernel_spmd

    arrays = {
        "x": np.ascontiguousarray(x).reshape(TOKENS, D),
        "ctx_rows": np.ascontiguousarray(ctx_1024),
        "ctx_cols": np.ascontiguousarray(
            np.asarray(ctx_1024).transpose(0, 2, 1).reshape(B, KD, P, CTX).transpose(0, 2, 1, 3)).reshape(B, P, KD * CTX),
        "small": np.ascontiguousarray(np.concatenate([
            np.asarray(L0_ffn_gate_w).reshape(E, KD, P).transpose(2, 1, 0).reshape(P, KD * E),
            np.tile(np.asarray(L0_ffn_gate_b), (P, 1)),
            np.asarray(L0_ffn_b1).reshape(E, KH, P).transpose(2, 0, 1).reshape(P, E * KH),
            np.tile(np.asarray(g_xattn), (P, 1)), np.tile(np.asarray(g_ffn), (P, 1))], axis=1)),
        "w1t": np.ascontiguousarray(
            np.asarray(L0_ffn_w1).reshape(E, H, KD, P).transpose(0, 3, 2, 1)).reshape(E, P, KD * H),
        "w2t": np.ascontiguousarray(
            np.asarray(L0_ffn_w2).reshape(E, D, KH, P).transpose(0, 3, 2, 1)).reshape(E, P, KH * D),
        "b2": np.ascontiguousarray(L0_ffn_b2).reshape(E * D),
    }
    nc = bacc.Bacc("TRN2", target_bir_lowering=False, num_devices=1)
    args = [nc.dram_tensor(f"in_{n}", a.shape, mybir.dt.from_np(a.dtype), kind="ExternalInput").ap()
            for n, a in arrays.items()]
    out = nc.dram_tensor("out_rows", (TOKENS, D), F32, kind="ExternalOutput").ap()
    gated_cross_attention_moe(nc, *args, out)
    result = run_bass_kernel_spmd(nc, [{f"in_{n}": a for n, a in arrays.items()}], core_ids=[0])
    return result.results[0]["out_rows"].reshape(B, S, D)
```

```python
from contextlib import ExitStack

import concourse.bass as bass
from concourse import mybir

P = 128
ALU = mybir.AluOpType
ACT = mybir.ActivationFunctionType
AX_X = mybir.AxisListType.X
F32 = mybir.dt.float32
BF16 = mybir.dt.bfloat16
I32 = mybir.dt.int32
U32 = mybir.dt.uint32

EPS = 1e-5
B, S, D = 8, 112, 256
CTX = 375
E, H = 8, 1024
TOKENS = B * S
KD, KH = D // P, H // P
CC, CR = 3, CTX // 3
ROW = D + 4
MEAN, VAR, RSTD, VEPS = D, D + 1, D + 2, D + 3
CHUNKS = TOKENS // P
WARM = 16
AHEAD = 4
EARLY = 3
BLOCKS = E + 1
MAX_OVER = CHUNKS - 1
SLOTS = CHUNKS * E
SMALL = KD * E + E + E * KH + 2
LEAST = -3.4e38
NOWHERE = 65536.0


def gated_cross_attention_moe(nc, x, ctx_rows, ctx_cols, small, w1t, w2t, b2, out):
    x2_dram = nc.dram_tensor("x2_rows", (TOKENS, ROW), F32, kind="Internal").ap()
    with ExitStack() as stack:
        def sb(name, shape, dt=F32):
            return stack.enter_context(nc.sbuf_tensor(name, shape, dt))

        def ps(name, shape):
            return stack.enter_context(nc.psum_tensor(name, shape, F32))

        def sem(name):
            return stack.enter_context(nc.semaphore(name))

        w1 = sb("w1", [P, E, KD * H])
        w2 = sb("w2", [P, E, KH * D])
        b2b = sb("b2b", [P, E * D])
        smalls = sb("smalls", [P, SMALL])
        gw, gb = smalls[:, 0:KD * E], smalls[:, KD * E:(KD + 1) * E]
        b1, gates = smalls[:, (KD + 1) * E:SMALL - 2], smalls[:, SMALL - 2:SMALL]
        tg = sb("tg", [P, 2])
        region = sb("region", [P, B * (KD * CTX + CC * D)])
        cxT = region[:, 0:B * KD * CTX].rearrange("p (b n) -> p b n", b=B)
        cx = region[:, B * KD * CTX:].rearrange("p (b n) -> p b n", b=B)
        hid = region[:, 0:2 * H].rearrange("p (q n) -> p q n", q=2)
        hidT = region[:, 2 * H:4 * H].rearrange("p (q k n) -> p q k n", q=2, k=KH)
        xg = region[:, 4 * H:4 * H + (BLOCKS + 2) * ROW].rearrange("p (j n) -> p j n", j=BLOCKS + 2)
        xgn = region[:, 7 * H:7 * H + 2 * D].rearrange("p (q n) -> p q n", q=2)
        xgT = region[:, 7 * H + 2 * D:7 * H + 4 * D].rearrange("p (q n) -> p q n", q=2)

        xn2 = w2[:, E - 1, :].rearrange("p (b n) -> p b n", b=B)
        gel = w1[:, E - 1, 0:2 * CC * S].rearrange("p (q n) -> p q n", q=2)
        pick_x = w1[:, E - 1, H:H + EARLY * P].rearrange("p (b n) -> p b n", b=EARLY)
        xn = w1[:, E - 2, 0:2 * D].rearrange("p (q n) -> p q n", q=2)

        x2 = sb("x2", [P, B, ROW])
        xnT = sb("xnT", [P, 2, KD * S])
        xn2T = sb("xn2T", [P, 2, KD * S])
        pick_r0 = sb("pick_r0", [P, B, P], BF16)
        pick_e0 = sb("pick_e0", [P, B, 2, E], BF16)
        stats = sb("stats", [P, 6])
        stats2 = sb("stats2", [P, 6])
        mv = sb("mv", [P, 2, 4])
        power = sb("power", [P, 1])
        eps = sb("eps", [P, 1])
        unused = sb("unused", [P, 2])

        ident = sb("ident", [P, P])
        tri = sb("tri", [P, S], BF16)
        ones = sb("ones", [P, P], BF16)
        iota_r = sb("iota_r", [P, P], BF16)
        iota_e = sb("iota_e", [P, E])
        iota_k = sb("iota_k", [P, SLOTS])
        iota_b = sb("iota_b", [P, B])
        iota_j = sb("iota_j", [P, MAX_OVER])
        row_1 = sb("row_1", [P, 1])
        upto = sb("upto", [P, E, E])

        lg = sb("lg", [P, B, E])
        cand = sb("cand", [P, B, E])
        mx = sb("mx", [P, B])
        first = sb("first", [P, B])
        oh = sb("oh", [P, B, E], BF16)
        rk = sb("rk", [P, B, E])
        rank = sb("rank", [P, B])
        is_e0 = sb("is_e0", [P, EARLY])
        mask_e0 = sb("mask_e0", [1, EARLY, E])
        room = sb("room", [1, 1])
        shift = sb("shift", [1, EARLY, E], BF16)
        cnt_shift = sb("cnt_shift", [1, E], BF16)
        rank_i = sb("rank_i", [P, B], I32)
        rmod = sb("rmod", [P, B])
        base = sb("base", [P, B], I32)
        key = sb("key", [P, B])
        pick_r = sb("pick_r", [P, B, P], BF16)
        pick_k = sb("pick_k", [P, B, 2 * SLOTS], BF16)
        id1 = sb("id1", [P, SLOTS])
        empty = sb("empty", [P, SLOTS])
        from_row0 = sb("from_row0", [P, E], U32)
        to_row0 = sb("to_row0", [P, E], U32)
        empty0 = sb("empty0", [P, E])
        from_row = sb("from_row", [P, SLOTS], U32)
        to_row = sb("to_row", [P, SLOTS], U32)
        from_over = sb("from_over", [P, 2], U32)
        to_over = sb("to_over", [P, 2], U32)
        flags = sb("flags", [P, E, MAX_OVER])
        over = sb("over", [P, E])
        cum2 = sb("cum2", [P, E, E])
        cum = sb("cum", [P, E])
        before = sb("before", [P, MAX_OVER, E])
        before_n = sb("before_n", [P, MAX_OVER, E])
        ej = sb("ej", [P, MAX_OVER])
        sj = sb("sj", [P, MAX_OVER])
        cj = sb("cj", [P, MAX_OVER])
        ctrl = sb("ctrl", [P, 2 * MAX_OVER + 1], I32)

        banks = [ps(f"bank{i}", [P, 512]) for i in range(8)]
        xnT_ps, xg0_ps, at_ps, xn2T_ps, lg_ps, rk_ps = (banks[i] for i in (0, 2, 3, 4, 6, 7))
        sc_ps = [banks[1], banks[5]]
        tok0_ps, tok_ps = banks[0], banks[1]
        cnt_ps = tok0_ps[:, E:2 * E]
        h_ps = banks[0:2]
        hT_ps = banks[2:6]
        y_ps, xgT_ps = banks[6], banks[7]
        y_over_ps = banks[7]

        x_in = [sem("x_in0"), sem("x_in1"), sem("x_in2"), sem("x_in4")]
        small_in, b2_in = sem("small_in"), sem("b2_in")
        cxT_in = [sem("cxT_in0"), sem("cxT_in1")]
        cx_in = [sem("cx_in0"), sem("cx_in1")]
        w1_in = [sem("w1_in0"), sem("w1_in1")]
        w2_in = [sem("w2_in0"), sem("w2_in1")]
        pool_step = sem("pool_step")
        ident_ok, consts_ok = sem("ident_ok"), sem("consts_ok")
        tg_ok, veps_ok = sem("tg_ok"), sem("veps_ok")
        s1_ok, stats_ok, rstd_ok, xn_ok = sem("s1_ok"), sem("stats_ok"), sem("rstd_ok"), sem("xn_ok")
        xnT_done, xnT_ok = sem("xnT_done"), sem("xnT_ok")
        sc_done, gel_ok = sem("sc_done"), sem("gel_ok")
        at_done, x2_ok = sem("at_done"), sem("x2_ok")
        s2_ok, stats2_ok, rstd2_ok, xn2_ok = sem("s2_ok"), sem("stats2_ok"), sem("rstd2_ok"), sem("xn2_ok")
        xn2T_done, xn2T_ok, lg_done = sem("xn2T_done"), sem("xn2T_ok"), sem("lg_done")
        x2_stored = sem("x2_stored")
        dve_step = sem("dve_step")
        lg_read, route_step, cand_ok = sem("lg_read"), sem("route_step"), sem("cand_ok")
        first_ok, oh_ok, is_e0_ok, empty0_ok = sem("first_ok"), sem("oh_ok"), sem("is_e0_ok"), sem("empty0_ok")
        rk_done, rank_read, rank_ok = sem("rk_done"), sem("rank_read"), sem("rank_ok")
        pick_x_ok, picks0_ok, placed = sem("pick_x_ok"), sem("picks0_ok"), sem("placed")
        room_ok, shift_ok, cnt_shift_ok = sem("room_ok"), sem("shift_ok"), sem("cnt_shift_ok")
        tok0_done, rows0_ok, to_rows0_ok = sem("tok0_done"), sem("rows0_ok"), sem("to_rows0_ok")
        picks_ok, tok_done, tok_read = sem("picks_ok"), sem("tok_done"), sem("tok_read")
        rows_ok, ctrl_ok = sem("rows_ok"), sem("ctrl_ok")
        cnt_read = sem("cnt_read")
        first_in = [sem("first_in0"), sem("first_in1")]
        xg_in = [sem("xg_in0"), sem("xg_in1")]
        late_in = sem("late_in")
        over_in = [sem("over_in0"), sem("over_in1")]
        over_idx = sem("over_idx")
        xgn_ok, xgT_done, xgT_ok = sem("xgn_ok"), sem("xgT_done"), sem("xgT_ok")
        h_done = sem("h_done")
        h0_ok, h1_ok = sem("h0_ok"), sem("h1_ok")
        hT_done = sem("hT_done")
        hTa_ok, hTd_ok = sem("hTa_ok"), sem("hTd_ok")
        y_done, base_ok, o_ok = sem("y_done"), sem("base_ok"), sem("o_ok")
        out_done = [sem("out_done0"), sem("out_done1")]

        block = stack.enter_context(nc.Block())

        @block.sync
        def _(sp):
            def load_context(b, q):
                sp.dma_start(cxT[:, b, :], ctx_cols[b]).then_inc(cxT_in[q], 16)
                sp.dma_start(cx[0:CR, b, :].rearrange("p (c d) -> p c d", c=CC),
                             ctx_rows[b].rearrange("(c p) d -> p c d", p=CR)).then_inc(cx_in[q], 16)

            def load_expert(e, q):
                sp.dma_start(w1[:, e, :], w1t[e]).then_inc(w1_in[q], 16)
                sp.dma_start(w2[:, e, :], w2t[e]).then_inc(w2_in[q], 16)

            def load_x(b, n):
                return sp.dma_start(x2[0:S, b:b + n, 0:D], x[b * S:(b + n) * S].rearrange("(b p) d -> p b d", p=S))

            load_x(0, 1).then_inc(x_in[0], 16)
            load_x(1, 1).then_inc(x_in[1], 16)
            load_context(0, 0)
            load_x(2, 2).then_inc(x_in[2], 16)
            load_context(1, 1)
            sp.wait_ge(cxT_in[0], 16)
            sp.wait_ge(cx_in[0], 16)
            load_context(2, 0)
            load_x(4, 4).then_inc(x_in[3], 16)
            sp.wait_ge(cxT_in[1], 16)
            sp.wait_ge(cx_in[1], 16)
            load_context(3, 1)
            with sp.Fori(2, B // 2) as t:
                for q in range(2):
                    sp.wait_ge(cxT_in[q], 16 * t)
                    sp.wait_ge(cx_in[q], 16 * t)
                    load_context(2 * t + q, q)
            load_expert(0, 0)
            sp.dma_start(b2b[:], b2.partition_broadcast(P)).then_inc(b2_in, 16)
            sp.dma_start(w1[:, 1, :], w1t[1]).then_inc(w1_in[1], 16)
            sp.wait_ge(xn2T_ok, B)
            sp.wait_ge(w1_in[0], 16)
            sp.dma_start(w1[:, 2, :], w1t[2]).then_inc(w1_in[0], 16)
            for q in range(2):
                sp.wait_ge(first_in[q], 16)
            sp.wait_ge(xg_in[0], 16)
            sp.wait_ge(xgT_done, 1)
            sp.wait_ge(xn2T_done, B)
            sp.dma_start(w2[:, 1, :], w2t[1]).then_inc(w2_in[1], 16)
            sp.wait_ge(w2_in[0], 16)
            sp.dma_start(w2[:, 2, :], w2t[2]).then_inc(w2_in[0], 16)
            sp.wait_ge(w1_in[1], 16)
            sp.dma_start(w1[:, 3, :], w1t[3]).then_inc(w1_in[1], 16)
            sp.wait_ge(w2_in[1], 16)
            sp.dma_start(w2[:, 3, :], w2t[3]).then_inc(w2_in[1], 16)
            with sp.Fori(2, E // 2) as t:
                for q in range(2):
                    sp.wait_ge(w1_in[q], 16 * t)
                    sp.wait_ge(w2_in[q], 16 * t)
                    load_expert(2 * t + q, q)

        @block.gpsimd
        def _(pool):
            pool.memset(ident[:], 0.0).then_inc(pool_step, 1)
            pool.wait_ge(pool_step, 1)
            pool.affine_select(out=ident[:], in_=ident[:], compare_op=ALU.not_equal, fill=1.0, base=0,
                               pattern=[[-1, P]], channel_multiplier=1).then_inc(ident_ok, 1)
            pool.memset(power[:], -0.5).then_inc(pool_step, 1)
            pool.memset(eps[:], EPS).then_inc(pool_step, 1)
            pool.memset(ones[:], 1.0).then_inc(pool_step, 1)
            pool.wait_ge(pool_step, 4)
            pool.affine_select(out=tri[:], in_=ones[:, 0:S], compare_op=ALU.is_gt, fill=0.0, base=0,
                               pattern=[[1, S]], channel_multiplier=-1).then_inc(consts_ok, 1)
            pool.iota(iota_r[:], [[1, P]], base=0, channel_multiplier=0,
                      allow_small_or_imprecise_dtypes=True).then_inc(consts_ok, 1)
            pool.iota(iota_e[:], [[-1, E]], base=E, channel_multiplier=0,
                      allow_small_or_imprecise_dtypes=True).then_inc(consts_ok, 1)
            pool.iota(iota_k[:], [[P, SLOTS]], base=-P * E, channel_multiplier=0,
                      allow_small_or_imprecise_dtypes=True).then_inc(consts_ok, 1)
            pool.iota(iota_b[:], [[1, B]], base=0, channel_multiplier=0,
                      allow_small_or_imprecise_dtypes=True).then_inc(consts_ok, 1)
            pool.iota(iota_j[:], [[1, MAX_OVER]], base=0, channel_multiplier=0,
                      allow_small_or_imprecise_dtypes=True).then_inc(consts_ok, 1)
            pool.iota(row_1[:], [[0, 1]], base=1, channel_multiplier=1,
                      allow_small_or_imprecise_dtypes=True).then_inc(consts_ok, 1)
            pool.memset(upto[:], 1.0).then_inc(pool_step, 1)
            pool.wait_ge(pool_step, 5)
            pool.affine_select(out=upto[:], in_=upto[:], compare_op=ALU.is_ge, fill=0.0, base=0,
                               pattern=[[1, E], [-1, E]], channel_multiplier=0).then_inc(consts_ok, 1)
            pool.memset(mask_e0[:], 0.0).then_inc(pool_step, 1)
            pool.wait_ge(pool_step, 6)
            pool.memset(mask_e0[:, :, 0:1], 1.0).then_inc(consts_ok, 1)
            veps = [0]

            def inverse_std(v):
                pool.tensor_tensor(v[:, 3:4], v[:, 1:2], eps[0:S, :], ALU.add).then_inc(veps_ok, 1)
                veps[0] += 1
                pool.wait_ge(veps_ok, veps[0])
                return pool.tensor_tensor(v[:, 2:3], v[:, 3:4], power[0:S, :], ALU.pow)

            def of_x(b):
                pool.wait_ge(stats_ok, b + 1)
                inverse_std(mv[0:S, b % 2, :]).then_inc(rstd_ok, 1)

            for b in range(AHEAD):
                of_x(b)
            for b in range(B):
                pool.wait_ge(stats2_ok, b + 1)
                inverse_std(x2[0:S, b, MEAN:]).then_inc(rstd2_ok, 1)
                if b + AHEAD < B:
                    of_x(b + AHEAD)

            def gather(to, idx):
                return pool.indirect_dma_start(
                    out=to, out_offset=None, in_=x2_dram, in_offset=bass.IndirectOffsetOnAxis(ap=idx, axis=0),
                    bounds_check=TOKENS - 1, oob_is_err=False)

            def scatter(rows, idx):
                return pool.indirect_dma_start(
                    out=out, out_offset=bass.IndirectOffsetOnAxis(ap=idx, axis=0), in_=rows, in_offset=None,
                    bounds_check=TOKENS - 1, oob_is_err=False)

            pool.wait_ge(x2_stored, 16 * B)
            pool.wait_ge(rows0_ok, 1)
            for e in (1, 2, 0, *range(3, E)):
                if e >= 4:
                    pool.wait_ge(xg_in[e % 2], 16 * (e // 2 - 1))
                landed = first_in[e] if e < 2 else xg_in[e % 2]
                gather(xg[:, e, :], from_row0[:, e:e + 1]).then_inc(landed, 16)

            pool.wait_ge(rows_ok, 1)
            gather(xg[:, E, :], from_row[:, E:E + 1]).then_inc(late_in, 16)
            pool.wait_ge(ctrl_ok, 1)
            n_over = pool.value_load(ctrl[0:1, 2 * MAX_OVER:2 * MAX_OVER + 1], min_val=0, max_val=MAX_OVER)

            def over_gather(m):
                q = (m + 1) % 2
                col = pool.value_load(ctrl[0:1, MAX_OVER + m:MAX_OVER + m + 1], min_val=0, max_val=SLOTS - 1)
                pool.tensor_copy(from_over[:, q:q + 1], from_row[:, bass.ds(col, 1)]).then_inc(over_idx, 1)
                pool.tensor_copy(to_over[:, q:q + 1], to_row[:, bass.ds(col, 1)]).then_inc(over_idx, 1)
                pool.wait_ge(over_idx, 2 * (m + 1))
                gather(xg[:, BLOCKS + q, :], from_over[:, q:q + 1]).then_inc(over_in[q], 16)

            for m in range(2):
                with pool.If(n_over > m):
                    over_gather(m)
            pool.wait_ge(to_rows0_ok, 1)
            for j in range(BLOCKS):
                pool.wait_ge(o_ok, j + 1)
                rows = to_row0[:, j:j + 1] if j < E else to_row[:, E:E + 1]
                scatter(xg[:, j, 0:D], rows).then_inc(out_done[0], 16)

            def over_scatter(m):
                with pool.If(n_over > m):
                    q = (m + 1) % 2
                    pool.wait_ge(o_ok, BLOCKS + 1 + m)
                    scatter(xg[:, BLOCKS + q, 0:D], to_over[:, q:q + 1]).then_inc(out_done[1], 16)
                    pool.wait_ge(out_done[1], 16 * (m + 1))
                    if m + 2 < MAX_OVER:
                        with pool.If(n_over > m + 2):
                            over_gather(m + 2)
                    if m + 1 < MAX_OVER:
                        over_scatter(m + 1)
                    pool.wait_ge(over_in[q], 16 * (m // 2 + 1))

            over_scatter(0)
            pool.wait_ge(out_done[0], 16 * BLOCKS)

        @block.scalar
        def _(act):
            act.dma_start(smalls[:], small).then_inc(small_in, 16)
            act.wait_ge(ident_ok, 1)
            act.activation(unused[:, 0:1], ident[:, 0:1], ACT.Tanh)
            act.wait_ge(small_in, 16)
            act.activation(tg[:], gates, ACT.Tanh).then_inc(tg_ok, 1)
            act.activation(unused[:, 1:2], ident[:, 0:1], ACT.Gelu_apprx_tanh)

            def xnT_copy(b):
                act.wait_ge(xnT_done, b + 1)
                act.activation(xnT[:, b % 2, :], xnT_ps[:, 0:KD * S], ACT.Copy).then_inc(xnT_ok, 1)

            def gelu(b):
                act.wait_ge(sc_done, b + 1)
                if b >= 2:
                    act.wait_ge(at_done, b - 1)
                act.activation(gel[0:CR, b % 2, :], sc_ps[b % 2][0:CR, 0:CC * S],
                               ACT.Gelu_apprx_tanh).then_inc(gel_ok, 1)

            def xn2T_copy(b, turned=xn2T_ps):
                act.wait_ge(rstd2_ok, b + 1)
                act.dma_start(x2_dram[b * S:(b + 1) * S, :], x2[0:S, b, :]).then_inc(x2_stored, 16)
                act.wait_ge(xn2T_done, b + 1)
                act.activation(xn2T[:, b % 2, :], turned[:, 0:KD * S], ACT.Copy).then_inc(xn2T_ok, 1)

            def expert_0():
                act.wait_ge(is_e0_ok, 1)
                for b in range(EARLY):
                    act.wait_ge(picks0_ok, b + 1)
                    act.activation(pick_x[0:S, b, :], pick_r0[0:S, b, :], ACT.Copy,
                                   scale=is_e0[0:S, b:b + 1]).then_inc(pick_x_ok, 1)

            def xgT_copy(j, q, turned=xgT_ps):
                act.wait_ge(xgT_done, j + 1)
                act.activation(xgT[:, q, :], turned[:, 0:D], ACT.Copy).then_inc(xgT_ok, 1)

            xnT_copy(0)
            xnT_copy(1)
            gelu(0)
            for b in range(B):
                if b + 1 < B:
                    gelu(b + 1)
                if b + 2 < B:
                    xnT_copy(b + 2)
                if b == B - 1:
                    expert_0()
                    xgT_copy(0, 0, xg0_ps)
                if b >= 1:
                    xn2T_copy(b - 1)
            xn2T_copy(B - 1, xnT_ps)

            def relu(j, q, e, later=True, pairs=(0, 2)):
                if later:
                    act.wait_ge(y_done, j - 1)
                for k in pairs:
                    act.wait_ge(hT_done, 4 * j + k + 1)
                    for r in range(2):
                        act.activation(hidT[:, q, 2 * k + r, :], hT_ps[k][:, r * P:(r + 1) * P], ACT.Relu,
                                       bias=b1[:, bass.ds(e * KH + 2 * k + r, 1)]).then_inc((hTa_ok, hTd_ok)[k % 2], 1)

            relu(0, 0, 0, later=False, pairs=range(4))
            xgT_copy(1, 1)
            relu(1, 1, 1, later=False)
            xgT_copy(2, 0)
            with act.Fori(1, E // 2) as t:
                for q in range(2):
                    j = 2 * t + q
                    relu(j, q, j)
                    xgT_copy(j + 1, 1 - q)
            relu(E, 0, 0)

            def h0_copy(m, q):
                act.wait_ge(h_done, 2 * m + 1)
                act.activation(hid[:, q, 0:H // 2], h_ps[0][:], ACT.Copy).then_inc(h0_ok, 1)

            act.wait_ge(ctrl_ok, 1)
            n_over = act.value_load(ctrl[0:1, 2 * MAX_OVER:2 * MAX_OVER + 1], min_val=0, max_val=MAX_OVER)
            with act.If(n_over > 0):
                xgT_copy(BLOCKS, 1)
                h0_copy(0, 1)
                relu(BLOCKS, 1, act.value_load(ctrl[0:1, 0:1], min_val=0, max_val=E - 1))

            def next_over(m, q):
                xgT_copy(BLOCKS + m + 1, 1 - q)
                h0_copy(m + 1, 1 - q)
                e = act.value_load(ctrl[0:1, bass.ds(m + 1, 1)], min_val=0, max_val=E - 1)
                relu(BLOCKS + m + 1, 1 - q, e)

            with act.If(n_over > 1):
                next_over(0, 1)
                with act.Fori(0, MAX_OVER // 2) as t:
                    for r in range(2):
                        with act.If(n_over > 2 * t + 2 + r):
                            next_over(2 * t + 1 + r, r)

        @block.vector
        def _(dve):
            def stats_x(b):
                dve.wait_ge(x_in[b if b < 2 else 2 + b // 4], 16)
                if b >= 2:
                    dve.wait_ge(xn_ok, b - 1)
                if b >= 1:
                    dve.wait_ge(stats_ok, b)
                dve.bn_stats(stats[0:S, :], x2[0:S, b, 0:D]).then_inc(s1_ok, 1)
                dve.wait_ge(s1_ok, b + 1)
                dve.bn_aggr(mv[0:S, b % 2, 0:2], stats[0:S, :]).then_inc(stats_ok, 1)

            def norm_x(b):
                if b >= 2:
                    dve.wait_ge(xnT_done, b - 1)
                dve.wait_ge(rstd_ok, b + 1)
                dve.tensor_scalar(xn[0:S, b % 2, :], x2[0:S, b, 0:D], mv[0:S, b % 2, 0:1], mv[0:S, b % 2, 2:3],
                                  ALU.subtract, ALU.mult).then_inc(xn_ok, 1)

            def add_attention(b):
                dve.wait_ge(at_done, b + 1)
                sums = at_ps if b < B - 1 else rk_ps
                dve.scalar_tensor_tensor(out=x2[0:S, b, 0:D], in0=sums[0:S, 0:D], scalar=tg[0:S, 0:1],
                                         in1=x2[0:S, b, 0:D], op0=ALU.mult, op1=ALU.add).then_inc(x2_ok, 1)

            def stats_x2(b):
                dve.wait_ge(x2_ok, b + 1)
                if b >= 1:
                    dve.wait_ge(stats2_ok, b)
                dve.bn_stats(stats2[0:S, :], x2[0:S, b, 0:D]).then_inc(s2_ok, 1)

            def join_x2(b):
                dve.wait_ge(s2_ok, b + 1)
                dve.bn_aggr(x2[0:S, b, MEAN:MEAN + 2], stats2[0:S, :]).then_inc(stats2_ok, 1)

            def residual(b):
                add_attention(b)
                stats_x2(b)
                join_x2(b)

            def norm_x2(b):
                dve.wait_ge(rstd2_ok, b + 1)
                dve.tensor_scalar(xn2[0:S, b, :], x2[0:S, b, 0:D], x2[0:S, b, MEAN:MEAN + 1],
                                  x2[0:S, b, RSTD:RSTD + 1], ALU.subtract, ALU.mult).then_inc(xn2_ok, 1)

            def largest(b):
                dve.wait_ge(lg_done, b + 1)
                dve.tensor_tensor_reduce(out=lg[0:S, b, :], in0=lg_ps[0:S, b * E:(b + 1) * E], in1=gb[0:S, :],
                                         scale=1.0, scalar=LEAST, op0=ALU.add, op1=ALU.max,
                                         accum_out=mx[0:S, b:b + 1]).then_inc(lg_read, 1)

            def candidates(b, group):
                dve.wait_ge(lg_read, group)
                dve.scalar_tensor_tensor(out=cand[0:S, b, :], in0=lg[0:S, b, :], scalar=mx[0:S, b:b + 1],
                                         in1=iota_e[0:S, :], op0=ALU.is_equal, op1=ALU.mult).then_inc(cand_ok, 1)

            def first_one(b, n, group):
                dve.wait_ge(cand_ok, group)
                dve.tensor_reduce(first[0:S, b:b + n], cand[0:S, b:b + n], AX_X, ALU.max).then_inc(first_ok, 1)

            def one_hot(b, n, group):
                dve.wait_ge(first_ok, group)
                dve.tensor_tensor(oh[0:S, b:b + n], iota_e[0:S, :].unsqueeze(1).to_broadcast([S, n, E]),
                                  first[0:S, b:b + n].unsqueeze(2).to_broadcast([S, n, E]),
                                  ALU.is_equal).then_inc(oh_ok, 1)

            def route_group():
                b, n = 0, 3
                dve.wait_ge(lg_done, n)
                dve.tensor_tensor(lg[0:S, b:b + n],
                                  lg_ps[0:S, b * E:(b + n) * E].rearrange("p (b e) -> p b e", b=n),
                                  gb[0:S, :].unsqueeze(1).to_broadcast([S, n, E]), ALU.add).then_inc(lg_read, 1)
                dve.wait_ge(lg_read, 1)
                dve.tensor_reduce(mx[0:S, b:b + n], lg[0:S, b:b + n], AX_X, ALU.max).then_inc(route_step, 1)
                dve.wait_ge(route_step, 1)
                dve.tensor_tensor(cand[0:S, b:b + n], lg[0:S, b:b + n],
                                  mx[0:S, b:b + n].unsqueeze(2).to_broadcast([S, n, E]),
                                  ALU.is_equal).then_inc(route_step, 1)
                dve.wait_ge(route_step, 2)
                dve.tensor_tensor(cand[0:S, b:b + n], cand[0:S, b:b + n],
                                  iota_e[0:S, :].unsqueeze(1).to_broadcast([S, n, E]), ALU.mult).then_inc(cand_ok, 1)
                first_one(b, n, 1)
                one_hot(b, n, 1)
                dve.tensor_scalar(is_e0[0:S, :], first[0:S, 0:EARLY], float(E), None,
                                  ALU.is_equal).then_inc(is_e0_ok, 1)

            def skip_room():
                dve.wait_ge(rk_done, 1)
                dve.tensor_scalar(room[:], rk_ps[0:1, B * E:B * E + 1], -1.0, float(P), ALU.mult,
                                  ALU.add).then_inc(room_ok, 1)
                dve.wait_ge(room_ok, 1)
                dve.tensor_scalar(shift[:], mask_e0[:], room[:], 0.0, ALU.mult, ALU.max).then_inc(shift_ok, 1)
                dve.wait_ge(shift_ok, 1)
                dve.scalar_tensor_tensor(out=cnt_shift[:], in0=mask_e0[:, 0, :], scalar=-float(P), in1=shift[:, 0, :],
                                         op0=ALU.mult, op1=ALU.add).then_inc(cnt_shift_ok, 1)

            def route(b):
                largest(b)
                candidates(b, b - 1)
                first_one(b, 1, b - 1)
                one_hot(b, 1, b - 1)

            def own_count(b, n, group):
                dve.wait_ge(rk_done, group)
                dve.tensor_tensor(rk[0:S, b:b + n], rk_ps[0:S, b * E:(b + n) * E].rearrange("p (b e) -> p b e", b=n),
                                  oh[0:S, b:b + n], ALU.mult).then_inc(rank_read, 1)

            def rank_of(b, n, group):
                dve.wait_ge(rank_read, group)
                dve.tensor_reduce(rank[0:S, b:b + n], rk[0:S, b:b + n], AX_X, ALU.add).then_inc(rank_ok, 1)

            def rank_one(b, group):
                dve.wait_ge(rk_done, group)
                dve.tensor_tensor_reduce(out=rk[0:S, b, :], in0=rk_ps[0:S, b * E:(b + 1) * E], in1=oh[0:S, b, :],
                                         scale=1.0, scalar=0.0, op0=ALU.mult, op1=ALU.add,
                                         accum_out=rank[0:S, b:b + 1]).then_inc(rank_ok, 1)

            def pick(b, group):
                dve.wait_ge(rank_ok, group)
                dve.tensor_scalar(pick_r0[0:S, b, :], iota_r[0:S, :], rank[0:S, b:b + 1], None,
                                  ALU.is_equal).then_inc(picks0_ok, 1)

            def place():
                b, n = 0, B
                dve.wait_ge(oh_ok, 6)
                dve.tensor_scalar(pick_e0[0:S, b:b + n, 0, :], oh[0:S, b:b + n], row_1[0:S, 0:1], None, ALU.mult)
                dve.scalar_tensor_tensor(out=pick_e0[0:S, b:b + n, 1, :], in0=oh[0:S, b:b + n], scalar=float(S),
                                         in1=iota_b[0:S, b:b + n].unsqueeze(2).to_broadcast([S, n, E]),
                                         op0=ALU.mult, op1=ALU.mult).then_inc(placed, 1)

            for b in range(0, AHEAD, 2):
                stats_x(b)
                stats_x(b + 1)
                norm_x(b)
                norm_x(b + 1)
            dve.wait_ge(tg_ok, 1)
            dve.wait_ge(consts_ok, 9)
            for b in range(B - 1):
                if b < B - 2:
                    residual(b)
                else:
                    add_attention(b)
                    pick(0, 1)
                    stats_x2(b)
                    pick(1, 1)
                    join_x2(b)
                    pick(2, 1)
                if b + AHEAD < B:
                    stats_x(b + AHEAD)
                if b == 4:
                    route_group()
                if b == 5:
                    skip_room()
                    own_count(0, 3, 1)
                    rank_of(0, 3, 1)
                    route(3)
                if b < B - 2:
                    norm_x2(b)
                if b + AHEAD < B:
                    norm_x(b + AHEAD)
            largest(4)
            candidates(4, 3)
            add_attention(7)
            first_one(4, 1, 3)
            stats_x2(7)
            one_hot(4, 1, 3)
            join_x2(7)
            norm_x2(6)
            largest(5)
            norm_x2(7)
            candidates(5, 4)
            first_one(5, 1, 4)
            one_hot(5, 1, 4)
            largest(6)
            candidates(6, 5)
            own_count(3, 3, 2)
            first_one(6, 1, 5)
            largest(7)
            one_hot(6, 1, 5)
            candidates(7, 6)
            rank_of(3, 3, 2)
            first_one(7, 1, 6)
            pick(3, 2)
            one_hot(7, 1, 6)
            pick(4, 2)
            place()
            rank_one(6, 3)
            rank_one(7, 3)
            pick(5, 2)
            pick(6, 3)
            pick(7, 4)

            dve.wait_ge(tok0_done, 1)
            dve.tensor_scalar(from_row0[:], tok0_ps[:, 0:E], -1.0, 0.0, ALU.add, ALU.max).then_inc(rows0_ok, 1)
            dve.tensor_scalar(empty0[:], tok0_ps[:, 0:E], 0.0, NOWHERE, ALU.is_equal, ALU.mult).then_inc(empty0_ok, 1)
            dve.wait_ge(empty0_ok, 1)
            dve.scalar_tensor_tensor(out=to_row0[:], in0=tok0_ps[:, 0:E], scalar=-1.0, in1=empty0[:], op0=ALU.add,
                                     op1=ALU.add).then_inc(to_rows0_ok, 1)

            steps = [0]

            def step(instruction):
                instruction.then_inc(dve_step, 1)
                steps[0] += 1
                dve.wait_ge(dve_step, steps[0])

            def over_control():
                for c in range(MAX_OVER):
                    last = dve.tensor_scalar(flags[:, :, c], cnt_ps, float(P * (c + 1)), None, ALU.is_gt)
                last.then_inc(cnt_read, 1)
                dve.wait_ge(cnt_read, 1)
                step(dve.tensor_reduce(over[:], flags[:], AX_X, ALU.add))
                step(dve.tensor_tensor(cum2[:], upto[:], over[:].unsqueeze(1).to_broadcast([P, E, E]), ALU.mult))
                step(dve.tensor_reduce(cum[:], cum2[:], AX_X, ALU.add))
                step(dve.tensor_tensor(before[:], cum[:].unsqueeze(1).to_broadcast([P, MAX_OVER, E]),
                                       iota_j[:].unsqueeze(2).to_broadcast([P, MAX_OVER, E]), ALU.is_le))
                step(dve.tensor_reduce(ej[:], before[:], AX_X, ALU.add))
                step(dve.tensor_tensor(before_n[:], before[:], over[:].unsqueeze(1).to_broadcast([P, MAX_OVER, E]),
                                       ALU.mult))
                step(dve.tensor_reduce(sj[:], before_n[:], AX_X, ALU.add))
                step(dve.scalar_tensor_tensor(out=cj[:], in0=iota_j[:], scalar=1.0, in1=sj[:], op0=ALU.add,
                                              op1=ALU.subtract))
                step(dve.scalar_tensor_tensor(out=cj[:], in0=ej[:], scalar=0.0, in1=cj[:], op0=ALU.is_equal,
                                              op1=ALU.add))
                dve.tensor_copy(ctrl[:, 0:MAX_OVER], ej[:])
                dve.scalar_tensor_tensor(out=ctrl[:, MAX_OVER:2 * MAX_OVER], in0=cj[:], scalar=float(E), in1=ej[:],
                                         op0=ALU.mult, op1=ALU.add)
                dve.tensor_copy(ctrl[:, 2 * MAX_OVER:2 * MAX_OVER + 1], cum[:, E - 1:E]).then_inc(ctrl_ok, 1)

            def over_picks():
                step(dve.tensor_copy(rank_i[0:S], rank[0:S]))
                step(dve.tensor_scalar(base[0:S], rank_i[0:S], 7, 7, ALU.arith_shift_right, ALU.logical_shift_left))
                dve.tensor_tensor(rmod[0:S], rank[0:S], base[0:S], ALU.subtract)
                step(dve.tensor_scalar(key[0:S], base[0:S], float(E), None, ALU.mult))
                step(dve.scalar_tensor_tensor(out=key[0:S], in0=first[0:S], scalar=-float(P), in1=key[0:S],
                                              op0=ALU.mult, op1=ALU.add))
                for b in range(B):
                    dve.tensor_scalar(pick_r[0:S, b, :], iota_r[0:S, :], rmod[0:S, b:b + 1], None, ALU.is_equal)
                step(dve.tensor_tensor(pick_k[0:S, :, 0:SLOTS],
                                       iota_k[0:S, :].unsqueeze(1).to_broadcast([S, B, SLOTS]),
                                       key[0:S, :].unsqueeze(2).to_broadcast([S, B, SLOTS]), ALU.is_equal))
                step(dve.tensor_tensor(pick_k[0:S, :, SLOTS:2 * SLOTS], pick_k[0:S, :, 0:SLOTS],
                                       iota_b[0:S, :].unsqueeze(2).to_broadcast([S, B, SLOTS]), ALU.mult))
                dve.tensor_scalar(pick_k[0:S, :, 0:SLOTS], pick_k[0:S, :, 0:SLOTS], row_1[0:S, 0:1], None,
                                  ALU.mult).then_inc(picks_ok, 1)

            def over_table():
                dve.wait_ge(tok_done, 1)
                step(dve.tensor_copy(id1[:], tok_ps[:, 0:SLOTS]))
                dve.scalar_tensor_tensor(out=id1[:], in0=tok_ps[:, SLOTS:2 * SLOTS], scalar=float(S), in1=id1[:],
                                         op0=ALU.mult, op1=ALU.add).then_inc(tok_read, 1)
                dve.wait_ge(tok_read, 1)
                dve.tensor_scalar(from_row[:], id1[:], -1.0, 0.0, ALU.add, ALU.max)
                step(dve.tensor_scalar(empty[:], id1[:], 0.0, NOWHERE, ALU.is_equal, ALU.mult))
                dve.scalar_tensor_tensor(out=to_row[:], in0=id1[:], scalar=-1.0, in1=empty[:], op0=ALU.add,
                                         op1=ALU.add).then_inc(rows_ok, 1)

            def norm_block(j, q, rows, later=True):
                if later:
                    dve.wait_ge(xgT_done, j - 1)
                dve.tensor_scalar(xgn[:, q, :], rows[:, 0:D], rows[:, MEAN:MEAN + 1], rows[:, RSTD:RSTD + 1],
                                  ALU.subtract, ALU.mult).then_inc(xgn_ok, 1)

            def relu_pair(j, q, e, k):
                dve.wait_ge(hT_done, 4 * j + k + 1)
                for r in range(2):
                    dve.tensor_scalar(hidT[:, q, 2 * k + r, :], hT_ps[k][:, r * P:(r + 1) * P],
                                      b1[:, bass.ds(e * KH + 2 * k + r, 1)], 0.0, ALU.add,
                                      ALU.max).then_inc(hTd_ok, 1)

            def relu(j, q, e):
                dve.wait_ge(y_done, j - 1)
                for k in (1, 3):
                    relu_pair(j, q, e, k)

            def bias_2(e, rows):
                dve.scalar_tensor_tensor(out=rows[:, 0:D], in0=b2b[:, bass.ds(e * D, D)], scalar=tg[:, 1:2],
                                         in1=rows[:, 0:D], op0=ALU.mult, op1=ALU.add).then_inc(base_ok, 1)

            def finish(j, rows, y=y_ps):
                dve.wait_ge(base_ok, j + 1)
                dve.wait_ge(y_done, j + 1)
                dve.scalar_tensor_tensor(out=rows[:, 0:D], in0=y[:, 0:D], scalar=tg[:, 1:2], in1=rows[:, 0:D],
                                         op0=ALU.mult, op1=ALU.add).then_inc(o_ok, 1)

            over_control()
            dve.wait_ge(first_in[1], 16)
            norm_block(1, 1, xg[:, 1, :], later=False)
            dve.wait_ge(xg_in[0], 16)
            norm_block(2, 0, xg[:, 2, :], later=False)
            over_picks()
            for k in (1, 3):
                relu_pair(1, 1, 1, k)
            dve.wait_ge(first_in[0], 16)
            dve.wait_ge(b2_in, 16)
            bias_2(0, xg[:, 0, :])
            finish(0, xg[:, 0, :])
            dve.wait_ge(xg_in[1], 16)
            norm_block(3, 1, xg[:, 3, :])
            over_table()
            with dve.Fori(0, E // 2 - 2) as t:
                for r in range(2):
                    j = 2 * t + r + 1
                    relu(j + 1, r, j + 1)
                    bias_2(j, xg[:, j, :])
                    finish(j, xg[:, j, :])
                    dve.wait_ge(xg_in[r], 16 * (t + 2))
                    norm_block(j + 3, r, xg[:, j + 3, :])
            relu(E - 2, 0, E - 2)
            bias_2(E - 3, xg[:, E - 3, :])
            finish(E - 3, xg[:, E - 3, :])
            dve.wait_ge(late_in, 16)
            norm_block(E, 0, xg[:, E, :])
            relu(E - 1, 1, E - 1)
            bias_2(E - 2, xg[:, E - 2, :])
            finish(E - 2, xg[:, E - 2, :])
            n_over = dve.value_load(ctrl[0:1, 2 * MAX_OVER:2 * MAX_OVER + 1], min_val=0, max_val=MAX_OVER)
            with dve.If(n_over > 0):
                dve.wait_ge(over_in[1], 16)
                norm_block(BLOCKS, 1, xg[:, BLOCKS + 1, :])
            relu(E, 0, 0)
            bias_2(E - 1, xg[:, E - 1, :])
            finish(E - 1, xg[:, E - 1, :])

            def h1_copy(m, q):
                dve.wait_ge(h_done, 2 * m + 2)
                dve.tensor_copy(hid[:, q, H // 2:H], h_ps[1][:]).then_inc(h1_ok, 1)

            with dve.If(n_over > 0):
                h1_copy(0, 1)
                relu(BLOCKS, 1, dve.value_load(ctrl[0:1, 0:1], min_val=0, max_val=E - 1))
            bias_2(0, xg[:, E, :])
            finish(E, xg[:, E, :], y_over_ps)

            def next_over(m, q, landed):
                dve.wait_ge(over_in[1 - q], 16 * landed)
                norm_block(BLOCKS + m + 1, 1 - q, xg[:, BLOCKS + 1 - q, :])
                h1_copy(m + 1, 1 - q)
                e = dve.value_load(ctrl[0:1, bass.ds(m + 1, 1)], min_val=0, max_val=E - 1)
                relu(BLOCKS + m + 1, 1 - q, e)

            def end_over(m, q):
                e = dve.value_load(ctrl[0:1, bass.ds(m, 1)], min_val=0, max_val=E - 1)
                bias_2(e, xg[:, BLOCKS + q, :])
                finish(BLOCKS + m, xg[:, BLOCKS + q, :], y_over_ps)

            with dve.If(n_over > 0):
                with dve.If(n_over > 1):
                    next_over(0, 1, 1)
                end_over(0, 1)
            with dve.If(n_over > 1):
                with dve.Fori(0, MAX_OVER // 2) as t:
                    for r in range(2):
                        m, q = 2 * t + 1 + r, r
                        with dve.If(n_over > m):
                            with dve.If(n_over > m + 1):
                                next_over(m, q, t + 2)
                            end_over(m, q)

        @block.tensor
        def _(pe):
            def turn_xn(b):
                pe.wait_ge(xn_ok, b + 1)
                if b >= 1:
                    pe.wait_ge(xnT_ok, b)
                for k in range(KD):
                    mm = pe.transpose(xnT_ps[:, k * S:(k + 1) * S], xn[0:S, b % 2, k * P:(k + 1) * P], ident[0:S, 0:S])
                mm.then_inc(xnT_done, 1)

            def scores(b):
                pe.wait_ge(xnT_ok, b + 1)
                pe.wait_ge(cxT_in[b % 2], 16 * (b // 2 + 1))
                if b >= 2:
                    pe.wait_ge(gel_ok, b - 1)
                for c in range(CC):
                    for k in range(KD):
                        mm = pe.matmul(sc_ps[b % 2][0:CR, c * S:(c + 1) * S],
                                       cxT[:, b, k * CTX + c * CR:k * CTX + (c + 1) * CR],
                                       xnT[:, b % 2, k * S:(k + 1) * S], start=(k == 0), stop=(k == KD - 1))
                mm.then_inc(sc_done, 1)

            def attend(b):
                pe.wait_ge(gel_ok, b + 1)
                pe.wait_ge(cx_in[b % 2], 16 * (b // 2 + 1))
                if 1 <= b < B - 1:
                    pe.wait_ge(x2_ok, b)
                if b == B - 1:
                    pe.wait_ge(rank_read, 1)
                for c in range(CC):
                    mm = pe.matmul((at_ps if b < B - 1 else rk_ps)[0:S, 0:D], gel[0:CR, b % 2, c * S:(c + 1) * S],
                                   cx[0:CR, b, c * D:(c + 1) * D], start=(c == 0), stop=(c == CC - 1))
                mm.then_inc(at_done, 1)

            def turn_xn2(b, to=xn2T_ps):
                pe.wait_ge(xn2_ok, b + 1)
                if 1 <= b < B - 1:
                    pe.wait_ge(xn2T_ok, b)
                for k in range(KD):
                    mm = pe.transpose(to[:, k * S:(k + 1) * S], xn2[0:S, b, k * P:(k + 1) * P],
                                      ident[0:S, 0:S])
                mm.then_inc(xn2T_done, 1)

            def logits(b):
                pe.wait_ge(xn2T_ok, b + 1)
                if b >= 3:
                    pe.wait_ge(lg_read, b - 2)
                for k in range(KD):
                    mm = pe.matmul(lg_ps[0:S, b * E:(b + 1) * E], xn2T[:, b % 2, k * S:(k + 1) * S],
                                   gw[:, k * E:(k + 1) * E], start=(k == 0), stop=(k == KD - 1))
                mm.then_inc(lg_done, 1)

            flat = oh[0:S].rearrange("p b e -> p (b e)")

            def same_batch(b, n, **flags):
                return pe.matmul(rk_ps[0:S, b * E:(b + n) * E], tri[0:S, :], flat[:, b * E:(b + n) * E], **flags)

            def batches_before(b, n, back, **flags):
                to = max(b, back)
                return pe.matmul(rk_ps[0:S, to * E:(b + n) * E], ones[0:S, 0:S],
                                 flat[:, (to - back) * E:(b + n - back) * E], **flags)

            def past_room(b, n):
                pe.wait_ge(shift_ok, 1)
                pe.matmul(rk_ps[0:S, b * E:(b + n) * E], ones[0:1, 0:S],
                          shift[:].rearrange("p b e -> p (b e)")[:, 0:n * E], start=False, stop=False)

            def rank_sums(b, n):
                same_batch(b, n, start=True, stop=False)
                if b >= EARLY:
                    past_room(b, n)
                for back in range(1, b + n):
                    mm = batches_before(b, n, back, start=False, stop=(back == b + n - 1))
                mm.then_inc(rk_done, 1)

            def first_block(b):
                for k in range(KD):
                    mm = pe.matmul(xg0_ps[:, k * P:(k + 1) * P], xn2[0:S, b, k * P:(k + 1) * P], pick_x[0:S, b, :],
                                   start=(b == 0 and k == 0), stop=(b == EARLY - 1 and k == KD - 1))
                return mm

            def tokens(b):
                for n in range(2):
                    mm = pe.matmul(tok0_ps[:, 0:E], pick_r0[0:S, b, :], pick_e0[0:S, b, n, :],
                                   start=(b == 0 and n == 0), stop=(b == B - 1 and n == 1))
                return mm

            def turn_block(j, q):
                pe.wait_ge(xgn_ok, j)
                for k in range(KD):
                    mm = pe.transpose(xgT_ps[:, k * P:(k + 1) * P], xgn[:, q, k * P:(k + 1) * P], ident[:])
                mm.then_inc(xgT_done, 1)

            def up(j, parts=range(KH)):
                e = j % E
                pe.wait_ge(xgT_ok, j + 1)
                pe.wait_ge(w1_in[e % 2], 16 * (e // 2 + 1))
                for part in parts:
                    k = part // 2
                    if part % 2 == 0 and j >= 1:
                        pe.wait_ge((hTa_ok, hTd_ok)[k % 2], 4 * (j - 1) + k // 2 * 2 + 2)
                    for n in range(KD):
                        mm = pe.matmul(hT_ps[k][:, part % 2 * P:(part % 2 + 1) * P],
                                       w1[:, e, n * H + part * P:n * H + (part + 1) * P],
                                       xgT[:, j % 2, n * P:(n + 1) * P], start=(n == 0), stop=(n == KD - 1))
                    if part % 2 == 1:
                        mm.then_inc(hT_done, 1)

            def down(j, q, e, parts=range(KH), y=y_ps):
                for part in parts:
                    pe.wait_ge((hTa_ok, hTd_ok)[part // 2 % 2], 4 * j + part // 4 * 2 + part % 2 + 1)
                    mm = pe.matmul(y[:, 0:D], hidT[:, q, part, :], w2[:, e, part * D:(part + 1) * D],
                                   start=(part == 0), stop=(part == KH - 1))
                if part == KH - 1:
                    mm.then_inc(y_done, 1)

            def keep_warm(n):
                for _ in range(n):
                    pe.transpose(sc_ps[0][:, 0:P], ident[:], ident[:])

            pe.wait_ge(ident_ok, 1)
            keep_warm(WARM)
            turn_xn(0)
            keep_warm(3)
            turn_xn(1)
            scores(0)
            pe.wait_ge(small_in, 16)
            for b in range(B):
                if b + 1 < B:
                    scores(b + 1)
                if b + 2 < B:
                    turn_xn(b + 2)
                attend(b)
                if 2 <= b < B - 1:
                    logits(b - 2)
                if 1 <= b < B - 1:
                    turn_xn2(b - 1)
                if b == 5:
                    pe.wait_ge(consts_ok, 9)
                    pe.wait_ge(oh_ok, 1)
                    for c in range(EARLY):
                        pe.matmul(rk_ps[0:1, B * E:(B + 1) * E], ones[0:S, 0:1], oh[0:S, c, :], start=(c == 0),
                                  stop=(c == EARLY - 1))
                    rank_sums(0, 3)
            for b in range(EARLY):
                pe.wait_ge(pick_x_ok, b + 1)
                mm = first_block(b)
            mm.then_inc(xgT_done, 1)
            logits(5)
            turn_xn2(6)
            up(0, (0,))
            logits(6)
            turn_xn2(7, xnT_ps)
            pe.wait_ge(oh_ok, 4)
            pe.wait_ge(x2_ok, B)
            rank_sums(3, 3)
            up(0, (1,))
            logits(7)
            up(0, (2, 3))
            pe.wait_ge(oh_ok, 6)
            pe.wait_ge(rank_read, 2)
            rank_sums(6, 2)
            pe.wait_ge(cnt_shift_ok, 1)
            for b in range(B):
                pe.matmul(cnt_ps, ones[0:S, :], oh[0:S, b, :], start=(b == 0), stop=False)
            pe.matmul(cnt_ps, ones[0:1, :], cnt_shift[:], start=False, stop=True)
            up(0, (4,))
            pe.wait_ge(placed, 1)
            for b in range(B):
                pe.wait_ge(picks0_ok, b + 1)
                mm = tokens(b)
            mm.then_inc(tok0_done, 1)
            up(0, (5, 6, 7))
            pe.wait_ge(w2_in[0], 16)
            down(0, 0, 0, range(0, KH - 2))
            turn_block(1, 1)
            down(0, 0, 0, range(KH - 2, KH))
            up(1, range(0, KH - 2))
            turn_block(2, 0)
            up(1, range(KH - 2, KH))
            up(2, range(0, KH // 2))
            pe.wait_ge(picks_ok, 1)
            for b in range(B):
                mm = pe.matmul(tok_ps[:, 0:2 * SLOTS], pick_r[0:S, b, :], pick_k[0:S, b, :],
                               start=(b == 0), stop=(b == B - 1))
            mm.then_inc(tok_done, 1)
            up(2, range(KH // 2, KH))
            for e in range(1, E - 1):
                if e >= 2:
                    up(e + 1)
                turn_block(e + 2, e % 2)
                pe.wait_ge(w2_in[e % 2], 16 * (e // 2 + 1))
                pe.wait_ge(o_ok, e)
                down(e, e % 2, e)

            def up_over(m, q, e, later=True):
                pe.wait_ge(xgT_ok, BLOCKS + m + 1)
                for n, read in enumerate((h0_ok, h1_ok)):
                    if later:
                        pe.wait_ge(read, m)
                    for k in range(KD):
                        mm = pe.matmul(h_ps[n][:], xgT[:, q, k * P:(k + 1) * P],
                                       w1[:, e, k * H + n * 512:k * H + (n + 1) * 512],
                                       start=(k == 0), stop=(k == KD - 1))
                    mm.then_inc(h_done, 1)

            def turn_hidden(m, q):
                pe.wait_ge(h0_ok, m + 1)
                pe.wait_ge(h1_ok, m + 1)
                pe.wait_ge(hTa_ok, 4 * (BLOCKS + m))
                pe.wait_ge(hTd_ok, 4 * (BLOCKS + m))
                for k in range(KH // 2):
                    for r in range(2):
                        mm = pe.transpose(hT_ps[k][:, r * P:(r + 1) * P],
                                          hid[:, q, (2 * k + r) * P:(2 * k + r + 1) * P], ident[:])
                    mm.then_inc(hT_done, 1)

            pe.wait_ge(ctrl_ok, 1)
            n_over = pe.value_load(ctrl[0:1, 2 * MAX_OVER:2 * MAX_OVER + 1], min_val=0, max_val=MAX_OVER)
            up(E)
            with pe.If(n_over > 0):
                turn_block(BLOCKS, 1)
            pe.wait_ge(w2_in[1], 16 * E // 2)
            pe.wait_ge(o_ok, E - 1)
            down(E - 1, 1, E - 1)
            with pe.If(n_over > 0):
                pe.wait_ge(cnt_read, 1)
                pe.wait_ge(tok_read, 1)
                up_over(0, 1, pe.value_load(ctrl[0:1, 0:1], min_val=0, max_val=E - 1), later=False)
            down(E, 0, 0, range(0, KH // 2), y_over_ps)
            with pe.If(n_over > 0):
                turn_hidden(0, 1)
            down(E, 0, 0, range(KH // 2, KH), y_over_ps)

            def next_over(m, q):
                turn_block(BLOCKS + m + 1, 1 - q)
                e = pe.value_load(ctrl[0:1, bass.ds(m + 1, 1)], min_val=0, max_val=E - 1)
                up_over(m + 1, 1 - q, e)
                turn_hidden(m + 1, 1 - q)

            def end_over(m, q):
                e = pe.value_load(ctrl[0:1, bass.ds(m, 1)], min_val=0, max_val=E - 1)
                down(BLOCKS + m, q, e, y=y_over_ps)

            with pe.If(n_over > 0):
                pe.wait_ge(o_ok, BLOCKS)
                with pe.If(n_over > 1):
                    next_over(0, 1)
                end_over(0, 1)
            with pe.If(n_over > 1):
                with pe.Fori(0, MAX_OVER // 2) as t:
                    for r in range(2):
                        m, q = 2 * t + 1 + r, r
                        with pe.If(n_over > m):
                            pe.wait_ge(o_ok, BLOCKS + m)
                            with pe.If(n_over > m + 1):
                                next_over(m, q)
                            end_over(m, q)


def kernel(x, ctx_1024, g_xattn, g_ffn, L0_ffn_gate_w, L0_ffn_gate_b, L0_ffn_w1, L0_ffn_b1, L0_ffn_w2, L0_ffn_b2):
    import numpy as np
    import concourse.bacc as bacc
    from concourse.bass_utils import run_bass_kernel_spmd

    arrays = {
        "x": np.ascontiguousarray(x).reshape(TOKENS, D),
        "ctx_rows": np.ascontiguousarray(ctx_1024),
        "ctx_cols": np.ascontiguousarray(
            np.asarray(ctx_1024).transpose(0, 2, 1).reshape(B, KD, P, CTX).transpose(0, 2, 1, 3)).reshape(B, P, KD * CTX),
        "small": np.ascontiguousarray(np.concatenate([
            np.asarray(L0_ffn_gate_w).reshape(E, KD, P).transpose(2, 1, 0).reshape(P, KD * E),
            np.tile(np.asarray(L0_ffn_gate_b), (P, 1)),
            np.asarray(L0_ffn_b1).reshape(E, KH, P).transpose(2, 0, 1).reshape(P, E * KH),
            np.tile(np.asarray(g_xattn), (P, 1)), np.tile(np.asarray(g_ffn), (P, 1))], axis=1)),
        "w1t": np.ascontiguousarray(
            np.asarray(L0_ffn_w1).reshape(E, H, KD, P).transpose(0, 3, 2, 1)).reshape(E, P, KD * H),
        "w2t": np.ascontiguousarray(
            np.asarray(L0_ffn_w2).reshape(E, D, KH, P).transpose(0, 3, 2, 1)).reshape(E, P, KH * D),
        "b2": np.ascontiguousarray(L0_ffn_b2).reshape(E * D),
    }
    nc = bacc.Bacc("TRN2", target_bir_lowering=False, num_devices=1)
    args = [nc.dram_tensor(f"in_{n}", a.shape, mybir.dt.from_np(a.dtype), kind="ExternalInput").ap()
            for n, a in arrays.items()]
    out = nc.dram_tensor("out_rows", (TOKENS, D), F32, kind="ExternalOutput").ap()
    gated_cross_attention_moe(nc, *args, out)
    result = run_bass_kernel_spmd(nc, [{f"in_{n}": a for n, a in arrays.items()}], core_ids=[0])
    return result.results[0]["out_rows"].reshape(B, S, D)
```
